# Optimizing a Trainium2 kernel written in Bass

```python
import numpy as np
import jax
import jax.numpy as jnp

def _softmax(x, axis=-1):
    return jax.nn.softmax(x, axis=axis)

def _gelu(x):
    return jax.nn.gelu(x, approximate=True)

def _silu(x):
    return jax.nn.silu(x)

def _sigmoid(x):
    return jax.nn.sigmoid(x)

def _layernorm(x, axis=-1, eps=1e-05):
    m = jnp.mean(x, axis=axis, keepdims=True)
    v = jnp.var(x, axis=axis, keepdims=True)
    return (x - m) / jnp.sqrt(v + eps)

def _scatter_add(tgt, idx, src, axis=0):
    return tgt.at[idx].add(src)

def _segment_sum(src, seg, n):
    return jax.ops.segment_sum(src, seg, n)
kernel_name = 'mk_gnn_resnorm_d1_gnn_r8_704003'

def setup_inputs(seed: int=0):
    np.random.seed(seed)
    _w = jnp.asarray

    def _rec_inputs():
        import jax
        import jax.numpy as jnp
        _gk = jax.random.key(seed)
        x = -0.0003713 + 1 * jax.random.normal(jax.random.fold_in(_gk, 1), (6250, 256), jnp.float32)
        src = jax.random.randint(jax.random.fold_in(_gk, 2), (200000,), 0, 6250, jnp.int32)
        dst = jnp.minimum((6250 * jax.random.uniform(jax.random.fold_in(_gk, 3), (200000,)) ** 2.0).astype(jnp.int32), 49999)
        _o = jnp.argsort(dst, stable=True)
        src = src[_o]
        dst = dst[_o]
        edge_type_8 = jax.random.randint(jax.random.fold_in(_gk, 12), (200000,), 0, 8, jnp.int32)
        return (x, src, dst, edge_type_8)
    x, src, dst, edge_type_8 = _rec_inputs()

    def _L0_gnn_setup():
        import jax, jax.numpy as jnp
        import numpy as np
        N_NODES = 6250
        N_EDGES = 37500
        N_REL = 8
        D = 256
        N_LAYERS = 3

        def _rgcn_layer(x, W, root, bias, src, dst, seg):
            agg = jax.ops.segment_sum(x[src], seg, num_segments=N_REL * N_NODES)
            agg = agg.reshape(N_REL, N_NODES, -1)
            return jnp.einsum('rnd,rde->ne', agg, W) + x @ root + bias
        key = jax.random.key(seed)
        k1, k2, k3, k4, k5 = jax.random.split(key, 5)
        x = jax.random.normal(k1, (N_NODES, D), dtype=jnp.float32)
        scale = 1.0 / np.sqrt(D)
        weights = jax.random.normal(k2, (N_LAYERS, N_REL, D, D), dtype=jnp.float32) * scale
        roots = jax.random.normal(k3, (N_LAYERS, D, D), dtype=jnp.float32) * scale
        biases = jnp.zeros((N_LAYERS, D), dtype=jnp.float32)
        edge_index = jax.random.randint(k4, (2, N_EDGES), 0, N_NODES, dtype=jnp.int64)
        edge_type = jax.random.randint(k5, (N_EDGES,), 0, N_REL, dtype=jnp.int64)
        return {'x': x, 'weights': weights, 'roots': roots, 'biases': biases, 'edge_index': edge_index, 'edge_type': edge_type}
    _L0_gnn_all = _L0_gnn_setup()
    _L0_gnn_in = {k: v for k, v in _L0_gnn_all.items() if k in ('weights', 'roots', 'biases')}
    del _L0_gnn_all
    return {'x': x, 'src': src, 'dst': dst, 'edge_type_8': edge_type_8, 'L0_gnn_weights': _L0_gnn_in['weights'], 'L0_gnn_roots': _L0_gnn_in['roots'], 'L0_gnn_biases': _L0_gnn_in['biases']}

def reference(x, src, dst, edge_type_8, L0_gnn_weights, L0_gnn_roots, L0_gnn_biases):
    import jax
    import jax.numpy as jnp

    def _L0_gnn_ref(x, weights, roots, biases, edge_index, edge_type):
        import jax, jax.numpy as jnp
        import numpy as np
        N_NODES = 6250
        N_EDGES = 37500
        N_REL = 8
        D = 256
        N_LAYERS = 3

        def _rgcn_layer(x, W, root, bias, src, dst, seg):
            agg = jax.ops.segment_sum(x[src], seg, num_segments=N_REL * N_NODES)
            agg = agg.reshape(N_REL, N_NODES, -1)
            return jnp.einsum('rnd,rde->ne', agg, W) + x @ root + bias
        src, dst = (edge_index[0], edge_index[1])
        seg = edge_type * N_NODES + dst
        h = x
        for l in range(N_LAYERS - 1):
            h = jax.nn.relu(_rgcn_layer(h, weights[l], roots[l], biases[l], src, dst, seg))
        h = jax.nn.sigmoid(_rgcn_layer(h, weights[-1], roots[-1], biases[-1], src, dst, seg))
        return h
    edge_index = jnp.stack([src, dst])
    x = _layernorm(x + _L0_gnn_ref(x, L0_gnn_weights, L0_gnn_roots, L0_gnn_biases, edge_index, edge_type_8), axis=-1)
    return x

_drawn_inputs = setup_inputs


def setup_inputs(seed=0):
    import zlib

    import numpy as np

    out = dict(_drawn_inputs(seed))
    spreads = {'L0_gnn_biases': (0.0, 0.1)}
    factors = {}
    for name, (base, spread) in spreads.items():
        noise = np.random.default_rng([zlib.crc32(name.encode()), seed]).standard_normal(out[name].shape)
        drawn = base * np.exp(spread * noise) if base else spread * noise
        out[name] = jnp.asarray(drawn.astype(out[name].dtype))
    for name, factor in factors.items():
        out[name] = (out[name] * factor).astype(out[name].dtype)
    return out
```

```python
import concourse.bass as bass
from concourse import mybir
from contextlib import ExitStack

F32 = mybir.dt.float32
I32 = mybir.dt.int32
ALU = mybir.AluOpType
ACT = mybir.ActivationFunctionType
AXX = mybir.AxisListType.X
ds = bass.ds

P = 128
SLOTS = 16
COLS = 512
NO_NODE = float(1 << 20)
FAR = 2048.0


def relational_graph_layers(nc, x, src, dst, edge_type, weights, roots, biases, out):
    N, D = x.shape
    E = src.shape[0]
    L, R = weights.shape[0], weights.shape[1]
    T = -(-N // P)
    LAST = N - (T - 1) * P
    C = -(-E // P)
    CB = -(-(C + SLOTS) // P)
    CP = CB * P
    FULL = E // P
    FB = FULL // P
    KD = D // P
    RD = R * D
    YG = RD // COLS
    HG = YG // 2
    EPS = 1e-5

    ctx = ExitStack()
    with ctx:
        def sb(name, shape, dt=F32):
            return ctx.enter_context(nc.sbuf_tensor(name, shape, dt))

        def sem(name):
            return ctx.enter_context(nc.semaphore(name))

        ytab = [nc.dram_tensor(f"ytab{i}", (T * P, RD), F32).ap() for i in range(2)]
        yrow = [y.rearrange("n (r e) -> (n r) e", e=D) for y in ytab]

        w_sb = sb("w_sb", [P, L, KD, RD])
        root_sb = sb("root_sb", [P, L, KD, D])
        bias_sb = sb("bias_sb", [1, L * D])
        hroot = sb("hroot", [P, T, D])
        rows_t = sb("rows_t", [P, CP], I32)
        dst_t = sb("dst_t", [P, CP])
        node_no = sb("node_no", [P, T * P])
        ident = sb("ident", [P, P])
        ones = sb("ones", [P, P])
        eps = sb("eps", [P, 1])
        plan = sb("plan", [1, (T + 1) * 2], I32)
        gath = sb("gath", [P, SLOTS, D])
        rowslot = sb("rowslot", [P, SLOTS], I32)
        hot = sb("hot", [P, 2, P])
        xin = sb("xin", [P, 2, D])
        h_sb = sb("h_sb", [P, D])
        h_t = sb("h_t", [P, 2, KD, P])
        ystage = sb("ystage", [P, RD])
        stats = sb("stats", [P, 6])
        mv = sb("mv", [P, 2])
        std = sb("std", [P, 1])
        rstd = sb("rstd", [P, 1])
        z_sb = sb("z_sb", [P, D])
        o_sb = sb("o_sb", [P, D])
        src_r = sb("src_r", [P, CP], I32)
        typ_r = sb("typ_r", [P, CP], I32)
        dst_r = sb("dst_r", [P, CP], I32)
        late = w_sb[:, 1:3, :, :].rearrange("p l k n -> p (l k n)")
        rows_f = late[:, 0:CP]
        dst_f = late[:, CP:2 * CP]
        dst_v = late[:, 2 * CP:3 * CP]
        spread_hi = dst_v
        reach_lo = rows_f
        reach = dst_f
        spread = late[:, 3 * CP:4 * CP]
        chunk_no = gath[:, :, :].rearrange("p s d -> p (s d)")[:, 0:CP]
        part_no = sb("part_no", [P, 1])
        lo = sb("lo", [P, 1])
        hi = sb("hi", [P, 1])
        dlow = sb("dlow", [P, CB])
        dhigh = sb("dhigh", [P, CB])
        tri = sb("tri", [P, P])
        v = sb("v", [P, 16])
        vi = sb("vi", [P, 4], I32)
        plan_c = sb("plan_c", [P, 2], I32)

        bank = [ctx.enter_context(nc.psum_tensor(f"bank{i}", [P, COLS], F32)) for i in range(8)]
        acc = bank[0]
        ps_t = [bank[1], bank[7]]
        ps_r = bank[2]
        ps_y = bank[3:3 + YG]

        consts_pool = sem("consts_pool")
        pads = sem("pads")
        edges_in = sem("edges_in")
        w0_in = sem("w0_in")
        late_in = sem("late_in")
        dve_step = sem("dve_step")
        edge_rows = sem("edge_rows")
        tr_ready = sem("tr_ready")
        tr_taken = sem("tr_taken")
        spread_ready = sem("spread_ready")
        span_ready = sem("span_ready")
        span_taken = sem("span_taken")
        steps_ready = sem("steps_ready")
        sum_ready = sem("sum_ready")
        plan_ready = sem("plan_ready")
        plan_in = sem("plan_in")
        x_in = [sem(f"x_in{i}") for i in range(2)]
        xt_done = sem("xt_done")
        ht_copied = sem("ht_copied")
        r_ready = sem("r_ready")
        r_taken = sem("r_taken")
        y_ready = sem("y_ready")
        y_taken = sem("y_taken")
        y_stored = [sem(f"y_stored{i}") for i in range(2)]
        slots_free = sem("slots_free")
        rows_ready = sem("rows_ready")
        gathered = [sem(f"gathered{i}") for i in range(SLOTS)]
        arrived = sem("arrived")
        hot_ready = sem("hot_ready")
        acc_ready = sem("acc_ready")
        acc_taken = sem("acc_taken")
        sig_done = sem("sig_done")
        res_in = sem("res_in")
        stats_done = sem("stats_done")      
        std_done = sem("std_done")
        o_ready = sem("o_ready")
        norm_step = sem("norm_step")
        res_done = sem("res_done")
        bn_done = sem("bn_done")
        o_stored = sem("o_stored")

        block = ctx.enter_context(nc.Block())

        def edge_view(a):
            return a[0:FB * P * P].rearrange("(b p e) -> p b e", p=P, e=P)

        def window(eng, t):
            first = eng.value_load(plan[0:1, ds(t * 2, 1)], min_val=0, max_val=T * CP)
            chunk = eng.value_load(plan[0:1, ds(t * 2 + 1, 1)], min_val=0, max_val=C - 1)
            after = eng.value_load(plan[0:1, ds(t * 2 + 2, 1)], min_val=2, max_val=T * CP)
            return first, chunk, after

        def column(c):
            return ds(nc.s_assert_within(c, 0, CP - 1, skip_runtime_bounds_check_because=(
                "a window's steps end at most SLOTS + 1 chunks past its last chunk")), 1)

        @block.sync
        def _(sp):
            sp.wait_ge(pads, 1)
            for raw, given in ((src_r, src), (typ_r, edge_type), (dst_r, dst)):
                sp.dma_start(raw[:, 0:FB * P].rearrange("p (b e) -> p b e", e=P),
                             edge_view(given)).then_inc(edges_in, 16)
                sp.dma_start(raw[0:FULL - FB * P, FB * P:(FB + 1) * P],
                             given[FB * P * P:FULL * P].rearrange("(p e) -> p e", e=P)).then_inc(edges_in, 16)
                sp.dma_start(raw[FULL - FB * P:FULL - FB * P + 1, FB * P:FB * P + E - FULL * P],
                             given[FULL * P:E].rearrange("(p e) -> p e", p=1)).then_inc(edges_in, 16)
            sp.dma_start(xin[:, 0, :], x[0:P, :]).then_inc(x_in[0], 16)
            sp.dma_start(w_sb[:, 0, :, :].rearrange("p k (r e) -> p k r e", e=D)[:, 0],
                         weights[0, :, 0:P, :].rearrange("r k e -> k r e")).then_inc(w0_in, 16)
            sp.dma_start(w_sb[:, 0, :, :].rearrange("p k (r e) -> p k r e", e=D)[:, 1],
                         weights[0, :, P:D, :].rearrange("r k e -> k r e")).then_inc(w0_in, 16)
            for l in range(L):
                sp.dma_start(root_sb[:, l, :, :], roots[l].rearrange("(k p) e -> p k e", p=P)).then_inc(w0_in, 16)
            sp.dma_start(bias_sb[:, :], biases.rearrange("(a l) e -> a (l e)", a=1)).then_inc(w0_in, 16)
            sp.dma_start(xin[:, 1, :], x[P:2 * P, :]).then_inc(x_in[1], 16)
            with sp.Fori(2, T - 2, 2) as t:
                for i in range(2):
                    sp.wait_ge(xt_done, t + i - 1)
                    sp.dma_start(xin[:, i, :], x[ds((t + i) * P, P), :]).then_inc(x_in[i], 16)
            sp.wait_ge(xt_done, T - 2)
            sp.dma_start(xin[0:LAST, 0, :], x[(T - 1) * P:N, :]).then_inc(x_in[0], 16)
            sp.wait_ge(plan_ready, 1)
            sp.dma_start(plan[0:1, :].rearrange("a (t k) -> a t k", k=2), plan_c[0:T + 1, :]).then_inc(plan_in, 16)
            for l in range(1, L):
                for k in range(KD):
                    sp.dma_start(w_sb[:, l, k, :].rearrange("p (r e) -> p r e", e=D),
                                 weights[l, :, k * P:(k + 1) * P, :].rearrange("r k e -> k r e")).then_inc(late_in, 16)
            sp.wait_ge(plan_in, 16)
            total = sp.value_load(plan[0:1, T * 2:T * 2 + 1], min_val=SLOTS, max_val=T * CP)
            for l in range(L):
                with sp.Fori(0, total, SLOTS) as s:
                    for i in range(SLOTS):
                        sp.wait_ge(gathered[i], total * l + s + 16)
                        sp.sem_inc(arrived, 1)

        @block.gpsimd
        def _(pool):
            pool.iota(part_no[:, :], [[0, 1]], base=0, channel_multiplier=1,
                      allow_small_or_imprecise_dtypes=True).then_inc(consts_pool, 1)
            pool.iota(node_no[:, :], [[1, T * P]], base=0, channel_multiplier=0,
                      allow_small_or_imprecise_dtypes=True).then_inc(consts_pool, 1)
            pool.iota(chunk_no, [[1, CP]], base=1, channel_multiplier=0,
                      allow_small_or_imprecise_dtypes=True).then_inc(consts_pool, 1)
            pool.wait_ge(plan_in, 16)
            total = pool.value_load(plan[0:1, T * 2:T * 2 + 1], min_val=SLOTS, max_val=T * CP)
            for l in range(L):
                pool.wait_ge(y_stored[0], 16 * T * (l + 1))
                pool.wait_ge(y_stored[1], 16 * T * (l + 1))
                with pool.Fori(0, total, SLOTS) as s:
                    for i in range(SLOTS):
                        pool.wait_ge(rows_ready, total * l + s + (i + 1))
                        pool.nop(nofuse=True)
                        pool.indirect_dma_start(
                            out=gath[:, i, :], out_offset=None, in_=yrow[l % 2],
                            in_offset=bass.IndirectOffsetOnAxis(ap=rowslot[:, i:i + 1], axis=0),
                        ).then_inc(gathered[i], 16)

        @block.scalar
        def _(act):
            def h_t_copy(n, i, again=True):
                act.wait_ge(xt_done, n + 1)
                if again:
                    act.wait_ge(y_ready, (n - 1) * YG)
                nc.scalar.copy(h_t[:, i, :, :].rearrange("p k m -> p (k m)"),
                               ps_t[i][:, 0:D]).then_inc(ht_copied, 1)

            def y_take(n, again=True):
                act.wait_ge(r_ready, n + 1)
                nc.scalar.copy(hroot[:, ds(n, 1), :], ps_r[:, 0:D]).then_inc(r_taken, 1)
                for half in range(2):
                    if again:
                        act.wait_ge(y_stored[half], n * 16)
                    for k in range(half * HG, (half + 1) * HG):
                        act.wait_ge(y_ready, n * YG + (k + 1))
                        nc.scalar.copy(ystage[:, k * COLS:(k + 1) * COLS], ps_y[k][:, :]).then_inc(y_taken, 1)
                    y_store(n, n, half, ytab[0])

            def y_store(n, t, half, table):
                act.wait_ge(y_taken, n * YG + (half + 1) * HG)
                w = HG * COLS
                act.dma_start(table[ds(t * P, P), half * w:(half + 1) * w],
                              ystage[:, half * w:(half + 1) * w]).then_inc(y_stored[half], 16)

            h_t_copy(0, 0, False)
            h_t_copy(1, 1, False)
            y_take(0, False)
            with act.Fori(1, T - 3, 2) as t:
                h_t_copy(t + 1, 0)
                y_take(t)
                h_t_copy(t + 2, 1)
                y_take(t + 1)
            h_t_copy(T - 1, 0)
            for t in (T - 2, T - 1):
                y_take(t)

            act.wait_ge(plan_in, 16)
            total = act.value_load(plan[0:1, T * 2:T * 2 + 1], min_val=SLOTS, max_val=T * CP)

            def name_rows(l, t):
                first, chunk, after = window(act, t)
                with act.Fori(0, after - first, 2) as k:
                    for j in range(2):
                        act.wait_ge(slots_free, total * l + first + k + (j + 1))
                        nc.scalar.copy(rowslot[:, ds((first + k + j) & (SLOTS - 1), 1)],
                                       rows_t[:, column(chunk + k + j)]).then_inc(rows_ready, 1)

            for l in range(L - 1):
                def store_both(t):
                    for half in range(2):
                        y_store((l + 1) * T + t, t, half, ytab[(l + 1) % 2])

                name_rows(l, 0)
                with act.Fori(1, T) as t:
                    name_rows(l, t)
                    store_both(t - 1)
                store_both(T - 1)

            def last_steps(t):
                def at(lag):
                    return not isinstance(t, int) or 0 <= t - lag < T

                if at(1):
                    rows = LAST if isinstance(t, int) and t - 1 == T - 1 else P
                    if not isinstance(t, int) or t >= 2:
                        act.wait_ge(stats_done, t - 1)
                    act.dma_start(xin[0:rows, 0, :], x[ds((t - 1) * P, rows), :]).then_inc(res_in, 16)
                    act.wait_ge(acc_taken, (L - 1) * T + t)
                    nc.scalar.activation(hroot[:, ds(t - 1, 1), :], hroot[:, ds(t - 1, 1), :],
                                         ACT.Sigmoid).then_inc(sig_done, 1)
                if at(2):
                    act.wait_ge(stats_done, t - 1)
                    nc.scalar.activation(std[:, :], mv[:, 1:2], ACT.Sqrt, bias=eps[:, 0:1]).then_inc(std_done, 1)
                if at(3):
                    rows = LAST if isinstance(t, int) and t - 3 == T - 1 else P
                    act.wait_ge(o_ready, t - 2)
                    act.dma_start(out[ds((t - 3) * P, rows), :], o_sb[0:rows, :]).then_inc(o_stored, 16)

            for t in range(4):
                name_rows(L - 1, t)
                last_steps(t)
            with act.Fori(4, T) as t:
                name_rows(L - 1, t)
                last_steps(t)
            for t in range(T, T + 3):
                last_steps(t)
            act.wait_ge(o_stored, 16 * T)

        @block.vector
        def _(dve):
            chain = [0]

            def link(made):
                chain[0] += 1
                made.then_inc(dve_step, 1)
                dve.wait_ge(dve_step, chain[0])

            V = nc.vector
            V.memset(src_r[:, FB * P:CP], 0)
            V.memset(typ_r[:, FB * P:CP], 0)
            V.memset(rowslot[:, :], 0)
            V.memset(ones[:, :], 1.0)
            V.memset(eps[:, :], EPS)
            link(V.memset(dst_r[:, FB * P:CP], int(NO_NODE)))
            dve.sem_inc(pads, 1)
            dve.wait_ge(consts_pool, 3)
            V.tensor_scalar(ident[:, :], node_no[:, 0:P], part_no[:, 0:1], None, ALU.is_equal)
            V.tensor_scalar(tri[:, :], node_no[:, 0:P], part_no[:, 0:1], None, ALU.is_ge)
            V.tensor_scalar(lo[:, :], part_no[:, :], float(P), None, ALU.mult)
            V.tensor_scalar(hi[:, :], part_no[:, :], float(P), float(P), ALU.mult, ALU.add)
            V.tensor_scalar(v[:, 7:8], part_no[:, :], float(T), None, ALU.is_lt)
            dve.wait_ge(edges_in, 9 * 16)
            V.scalar_tensor_tensor(rows_f, src_r[:, :], float(R), typ_r[:, :], ALU.mult, ALU.add)
            link(V.tensor_copy(dst_f, dst_r[:, :]))
            dve.sem_inc(edge_rows, 1)
            link(V.scalar_tensor_tensor(dst_v, dst_f, NO_NODE / 2, dst_f, ALU.is_lt, ALU.mult))
            by_chunk = "p (b e) -> p b e"
            V.tensor_reduce(dlow[:, :], dst_f.rearrange(by_chunk, e=P), AXX, ALU.min)
            link(V.tensor_reduce(dhigh[:, :], dst_v.rearrange(by_chunk, e=P), AXX, ALU.max))
            for end, made in ((dlow, spread), (dhigh, spread_hi)):
                V.tensor_tensor(made.rearrange(by_chunk, e=P), ident[:, :].unsqueeze(1).broadcast_to([P, CB, P]),
                                end[:, :].unsqueeze(2).broadcast_to([P, CB, P]), ALU.mult).then_inc(spread_ready, 1)
            for i, to in enumerate((rows_t, dst_t)):
                for b in range(4):
                    dve.wait_ge(tr_ready, 4 * i + b + 1)
                    w = min(COLS, CP - b * COLS)
                    V.tensor_copy(to[:, b * COLS:b * COLS + w], bank[4 * i + b][:, 0:w]).then_inc(tr_taken, 1)
            for b in range(4):
                dve.wait_ge(span_ready, b + 1)
                w = min(COLS, CP - b * COLS)
                V.tensor_scalar(reach_lo[:, b * COLS:b * COLS + w], bank[b][:, 0:w], hi[:, 0:1], None,
                                ALU.is_lt).then_inc(span_taken, 1)
            dve.wait_ge(span_taken, 4)
            for b in range(4):
                dve.wait_ge(span_ready, b + 5)
                w = min(COLS, CP - b * COLS)
                V.scalar_tensor_tensor(reach[:, b * COLS:b * COLS + w], bank[4 + b][:, 0:w], lo[:, 0:1],
                                       reach_lo[:, b * COLS:b * COLS + w], ALU.is_ge, ALU.mult).then_inc(span_taken, 1)
            dve.wait_ge(span_taken, 8)
            link(V.tensor_tensor(reach_lo, reach, chunk_no, ALU.mult))
            link(V.tensor_reduce(v[:, 0:1], reach_lo, AXX, ALU.max))
            link(V.tensor_scalar(spread, chunk_no, -1.0, FAR + 1, ALU.mult, ALU.add))
            link(V.tensor_tensor(reach_lo, reach, spread, ALU.mult))
            link(V.tensor_reduce(v[:, 1:2], reach_lo, AXX, ALU.max))
            link(V.tensor_scalar(v[:, 3:4], v[:, 1:2], -1.0, FAR, ALU.mult, ALU.add))
            link(V.tensor_scalar(v[:, 2:3], v[:, 3:4], float(C - 1), None, ALU.min))
            link(V.scalar_tensor_tensor(v[:, 4:5], v[:, 0:1], -1.0, v[:, 2:3], ALU.add, ALU.max))
            link(V.scalar_tensor_tensor(v[:, 5:6], v[:, 4:5], 2.0, v[:, 2:3], ALU.add, ALU.subtract))
            link(V.tensor_copy(vi[:, 0:1], v[:, 5:6]))
            link(V.tensor_scalar(vi[:, 1:2], vi[:, 0:1], 1, 1, ALU.arith_shift_right, ALU.arith_shift_left))
            link(V.tensor_copy(v[:, 6:7], vi[:, 1:2]))
            link(V.tensor_tensor(v[:, 8:9], v[:, 6:7], v[:, 7:8], ALU.mult))
            dve.sem_inc(steps_ready, 1)
            dve.wait_ge(sum_ready, 1)
            link(V.tensor_tensor(v[:, 9:10], acc[:, 0:1], v[:, 8:9], ALU.subtract))
            link(V.tensor_scalar(vi[:, 2:3], v[:, 9:10], float(SLOTS - 1), None, ALU.add))
            link(V.tensor_scalar(vi[:, 3:4], vi[:, 2:3], 4, 4, ALU.arith_shift_right, ALU.arith_shift_left))
            link(V.tensor_copy(v[:, 11:12], vi[:, 3:4]))
            link(V.tensor_tensor(v[:, 13:14], v[:, 11:12], v[:, 9:10], ALU.subtract))
            link(V.tensor_scalar(v[:, 12:13], v[:, 7:8], -1.0, 1.0, ALU.mult, ALU.add))
            link(V.tensor_tensor(v[:, 14:15], v[:, 13:14], v[:, 12:13], ALU.mult))
            V.tensor_tensor(plan_c[:, 0:1], v[:, 14:15], v[:, 9:10], ALU.add)
            link(V.tensor_copy(plan_c[:, 1:2], v[:, 2:3]))
            dve.sem_inc(plan_ready, 1)

            dve.wait_ge(plan_in, 16)
            total = dve.value_load(plan[0:1, T * 2:T * 2 + 1], min_val=SLOTS, max_val=T * CP)

            def one_hots(l, t):
                first, chunk, after = window(dve, t)
                with dve.Fori(0, after - first, 2) as k:
                    for j in range(2):
                        dve.wait_ge(slots_free, total * l + first + k + (j + SLOTS - 1))
                        V.tensor_scalar(hot[:, j, :], node_no[:, ds(t * P, P)], dst_t[:, column(chunk + k + j)],
                                        None, ALU.is_equal).then_inc(hot_ready, 1)

            for l in range(L - 1):
                with dve.Fori(0, T) as t:
                    one_hots(l, t)
                    n = (l + 1) * T + t
                    dve.wait_ge(acc_ready, l * T + t + 1)
                    V.tensor_scalar(h_sb[:, :], acc[:, 0:D], 0.0, None, ALU.max).then_inc(acc_taken, 1)
                    dve.wait_ge(xt_done, n + 1)
                    V.tensor_copy(h_t[:, 0, :, :].rearrange("p k m -> p (k m)"), ps_t[0][:, 0:D]).then_inc(ht_copied, 1)
                    dve.wait_ge(r_ready, n + 1)
                    V.tensor_copy(hroot[:, ds(t, 1), :], ps_r[:, 0:D]).then_inc(r_taken, 1)
                    for half in range(2):
                        dve.wait_ge(y_stored[half], n * 16)
                        for k in range(half * HG, (half + 1) * HG):
                            dve.wait_ge(y_ready, n * YG + (k + 1))
                            V.tensor_copy(ystage[:, k * COLS:(k + 1) * COLS], ps_y[k][:, :]).then_inc(y_taken, 1)

            def last_steps(t):
                def at(lag):
                    return not isinstance(t, int) or 0 <= t - lag < T

                if at(0):
                    dve.wait_ge(acc_ready, (L - 1) * T + t + 1)
                    V.tensor_copy(hroot[:, ds(t, 1), :], acc[:, 0:D]).then_inc(acc_taken, 1)
                if at(2):
                    dve.wait_ge(std_done, t - 1)
                    if not isinstance(t, int) or t >= 3:
                        dve.wait_ge(o_stored, 16 * (t - 2))
                    V.reciprocal(rstd[:, :], std[:, :]).then_inc(norm_step, 1)
                    dve.wait_ge(norm_step, t - 1)
                    V.tensor_scalar(o_sb[:, :], z_sb[:, :], mv[:, 0:1],
                                    rstd[:, 0:1], ALU.subtract, ALU.mult).then_inc(o_ready, 1)
                if at(1):
                    dve.wait_ge(sig_done, t)
                    dve.wait_ge(res_in, 16 * t)
                    if not isinstance(t, int) or t >= 2:
                        dve.wait_ge(o_ready, t - 1)
                    V.tensor_tensor(z_sb[:, :], hroot[:, ds(t - 1, 1), :].rearrange("p a d -> p (a d)"),
                                    xin[:, 0, :], ALU.add).then_inc(res_done, 1)
                    dve.wait_ge(res_done, t)
                    V.bn_stats(stats[:, :], z_sb[:, :]).then_inc(bn_done, 1)
                    dve.wait_ge(bn_done, t)
                    dve.nop(nofuse=True)
                    V.bn_aggr(mv[:, :], stats[:, :]).then_inc(stats_done, 1)

            for t in range(3):
                one_hots(L - 1, t)
                last_steps(t)
            with dve.Fori(3, T) as t:
                one_hots(L - 1, t)
                last_steps(t)
            for t in range(T, T + 2):
                last_steps(t)

        @block.tensor
        def _(pe):
            mm = nc.tensor.matmul
            pe.sem_inc(slots_free, SLOTS)
            pe.wait_ge(edge_rows, 1)
            for i, given in enumerate((rows_f, dst_f)):
                for b in range(CB):
                    made = nc.tensor.transpose(bank[4 * i + b // 4][:, (b % 4) * P:(b % 4 + 1) * P],
                                               given[:, b * P:(b + 1) * P], ident[:, :])
                    if b % 4 == 3 or b == CB - 1:
                        made.then_inc(tr_ready, 1)
            pe.wait_ge(tr_taken, 8)
            for i, given in enumerate((spread, spread_hi)):
                pe.wait_ge(spread_ready, i + 1)
                for b in range(4):
                    w = min(COLS, CP - b * COLS)
                    mm(bank[4 * i + b][:, 0:w], lhsT=ones[:, :], rhs=given[:, b * COLS:b * COLS + w],
                       start=True, stop=True).then_inc(span_ready, 1)
            pe.wait_ge(span_taken, 8)
            pe.wait_ge(w0_in, 16 * (KD + L + 1))

            def transposed(given, i):
                for k in range(KD):
                    made = nc.tensor.transpose(ps_t[i][:, k * P:(k + 1) * P], given[:, k * P:(k + 1) * P], ident[:, :])
                made.then_inc(xt_done, 1)

            def x_tile(n, i, again=True):
                pe.wait_ge(x_in[i], 8 * (n - i) + 16)
                if again:
                    pe.wait_ge(ht_copied, n - 1)
                transposed(xin[:, i, :], i)

            def products(n, i, l, again=True):
                pe.wait_ge(ht_copied, n + 1)
                if again:
                    pe.wait_ge(r_taken, n)
                for k in range(KD):
                    made = mm(ps_r[:, 0:D], lhsT=h_t[:, i, k, :], rhs=root_sb[:, l, k, :],
                              start=(k == 0), stop=(k == KD - 1))
                made.then_inc(r_ready, 1)
                for g in range(YG):
                    if again:
                        pe.wait_ge(y_taken, n * YG + (g + 1 - YG))
                    for k in range(KD):
                        made = mm(ps_y[g][:, :], lhsT=h_t[:, i, k, :], rhs=w_sb[:, l, k, g * COLS:(g + 1) * COLS],
                                  start=(k == 0), stop=(k == KD - 1))
                    made.then_inc(y_ready, 1)

            x_tile(0, 0, False)
            x_tile(1, 1, False)
            products(0, 0, 0, False)
            pe.wait_ge(steps_ready, 1)
            mm(acc[:, 0:1], lhsT=tri[:, :], rhs=v[:, 8:9], start=True, stop=True).then_inc(sum_ready, 1)
            with pe.Fori(1, T - 3, 2) as t:
                x_tile(t + 1, 0)
                products(t, 1, 0)
                x_tile(t + 2, 1)
                products(t + 1, 0, 0)
            x_tile(T - 1, 0)
            products(T - 2, 1, 0)
            products(T - 1, 0, 0)

            pe.wait_ge(plan_in, 16)
            total = pe.value_load(plan[0:1, T * 2:T * 2 + 1], min_val=SLOTS, max_val=T * CP)
            for l in range(L):
                with pe.Fori(0, T) as t:
                    first, chunk, after = window(pe, t)
                    if l == L - 1:
                        pe.wait_ge(acc_taken, l * T + t)
                    pe.wait_ge(r_taken, l * T + t + 1)
                    mm(acc[:, 0:D], lhsT=ident[:, :], rhs=hroot[:, ds(t, 1), :].rearrange("p a d -> p (a d)"),
                       start=True, stop=False)
                    with pe.Fori(0, after - first, 2) as k:
                        for j in range(2):
                            pe.wait_ge(hot_ready, total * l + first + k + (j + 1))
                            pe.wait_ge(arrived, total * l + first + k + (j + 1))
                            mm(acc[:, 0:D], lhsT=hot[:, j, :],
                               rhs=gath[:, ds((first + k + j) & (SLOTS - 1), 1), :].rearrange("p a d -> p (a d)"),
                               start=False, stop=False).then_inc(slots_free, 1)
                    mm(acc[:, 0:D], lhsT=ones[0:1, :], rhs=bias_sb[0:1, l * D:(l + 1) * D],
                       start=False, stop=True).then_inc(acc_ready, 1)
                    if l < L - 1:
                        if l == 0:
                            pe.wait_ge(late_in, 16 * (L - 1) * KD)
                        pe.wait_ge(acc_taken, l * T + t + 1)
                        transposed(h_sb, 0)
                        products((l + 1) * T + t, 0, l + 1)


_INS = ['x', 'src', 'dst', 'edge_type_8', 'L0_gnn_weights', 'L0_gnn_roots', 'L0_gnn_biases']


def kernel(**inputs):
    import numpy as _np
    import concourse.bacc as _bacc
    from concourse import mybir as _mybir
    from concourse.bass_utils import run_bass_kernel_spmd as _run

    nc = _bacc.Bacc("TRN2", target_bir_lowering=False, num_devices=1)
    arrays, args = {}, []
    for name in _INS:
        a = _np.ascontiguousarray(inputs[name])
        arrays[f"in_{name}"] = a
        args.append(nc.dram_tensor(f"in_{name}", a.shape, _mybir.dt.from_np(a.dtype), kind="ExternalInput").ap())
    out = nc.dram_tensor("out_0", inputs['x'].shape, _mybir.dt.float32, kind="ExternalOutput").ap()
    relational_graph_layers(nc, *args, out)
    r = _run(nc, [arrays], core_ids=[0])
    return r.results[0]["out_0"]
```

```python
import concourse.bass as bass
from concourse import mybir
from contextlib import ExitStack

F32 = mybir.dt.float32
I32 = mybir.dt.int32
ALU = mybir.AluOpType
ACT = mybir.ActivationFunctionType
AXX = mybir.AxisListType.X
ds = bass.ds

P = 128
SLOTS = 32
PAIRS = SLOTS // 2
LOG_PAIRS = PAIRS.bit_length() - 1
PLAN = 8
COLS = 512
NO_NODE = float(1 << 20)
FAR = 2048.0


def relational_graph_layers(nc, x, src, dst, edge_type, weights, roots, biases, out):
    N, D = x.shape
    E = src.shape[0]
    L, R = weights.shape[0], weights.shape[1]
    T = -(-N // P)
    LAST = N - (T - 1) * P
    C = -(-E // P)
    CB = -(-(C + SLOTS + 7) // P)
    CP = CB * P
    FULL = E // P
    FB = FULL // P
    KD = D // P
    RD = R * D
    YG = RD // COLS
    HG = YG // 2
    EPS = 1e-5

    ctx = ExitStack()
    with ctx:
        def sb(name, shape, dt=F32):
            return ctx.enter_context(nc.sbuf_tensor(name, shape, dt))

        def sem(name):
            return ctx.enter_context(nc.semaphore(name))

        ytab = [nc.dram_tensor(f"ytab{i}", (T * P, RD), F32).ap() for i in range(2)]
        yrow = [y.rearrange("n (r e) -> (n r) e", e=D) for y in ytab]

        w_sb = sb("w_sb", [P, L, KD, RD])
        root_sb = sb("root_sb", [P, L, KD, D])
        bias_sb = sb("bias_sb", [1, L * D])
        hroot = sb("hroot", [P, T, D])
        rows_t = sb("rows_t", [P, CP], I32)
        dst_t = sb("dst_t", [P, CP])
        node_no = sb("node_no", [P, T * P])
        ident = sb("ident", [P, P])
        ones = sb("ones", [P, P])
        nought = sb("nought", [1, D], mybir.dt.bfloat16)
        bias_all = sb("bias_all", [P, L, D])
        eps = sb("eps", [P, 1])
        plan = sb("plan", [1, (T + 1) * PLAN], I32)
        gath = sb("gath", [P, SLOTS, D])
        gath_flat = gath[:, :, :].rearrange("p s d -> p (s d)")
        rowslot = sb("rowslot", [P, SLOTS], I32)
        hot = sb("hot", [P, 4, P])
        xin = sb("xin", [P, 2, D])
        h_sb = sb("h_sb", [P, D])
        s_sb = sb("s_sb", [P, D])
        h_t = sb("h_t", [P, 2, KD, P])
        ystage = sb("ystage", [P, RD])
        stats = sb("stats", [P, 6])
        mv = sb("mv", [P, 2])
        std = sb("std", [P, 1])
        rstd = sb("rstd", [P, 1])
        z_sb = sb("z_sb", [P, D])
        o_sb = sb("o_sb", [P, D])
        late = w_sb[:, 1:3, :, :].rearrange("p l k n -> p (l k n)")
        rows_f = late[:, 0:CP]
        dst_f = late[:, CP:2 * CP]
        dst_v = late[:, 2 * CP:3 * CP]
        spread_hi = dst_v
        reach_lo = rows_f
        reach = dst_f
        spread = late[:, 3 * CP:4 * CP]
        chunk_no = gath_flat[:, 0:CP]
        src_r, typ_r, dst_r = (gath_flat[:, i * CP:(i + 1) * CP].bitcast(I32) for i in range(1, 4))
        part_no = sb("part_no", [P, 1])
        lo = sb("lo", [P, 1])
        hi = sb("hi", [P, 1])
        dlow = sb("dlow", [P, CB])
        dhigh = sb("dhigh", [P, CB])
        tri = sb("tri", [P, P])
        shift = sb("shift", [P, P])
        v = {name: sb(name, [P, 1]) for name in (
            "last_1", "from_end", "first_far", "first", "last", "is_window", "is_last", "first_quad",
            "last_quad", "quads", "same", "many", "share", "end", "end_up", "start", "twice")}
        vi = {name: sb(name, [P, 1], I32) for name in ("i0", "i1", "i2", "i3", "i4", "i5")}
        part_1 = sb("part_1", [P, 1])
        next_quad = sb("next_quad", [P, 1])
        counts = sb("counts", [P, 2])
        plan_c = sb("plan_c", [P, PLAN], I32)

        bank = [ctx.enter_context(nc.psum_tensor(f"bank{i}", [P, COLS], F32)) for i in range(8)]
        acc = bank[0]
        ps_t = [bank[1], bank[7]]
        ps_r = bank[2]
        ps_y = bank[3:3 + YG]

        consts_pool = sem("consts_pool")
        pads = sem("pads")
        edges_in = sem("edges_in")
        w0_in = sem("w0_in")
        late_in = sem("late_in")
        dve_step = sem("dve_step")
        edge_rows = sem("edge_rows")
        tr_ready = sem("tr_ready")
        tr_taken = sem("tr_taken")
        spread_ready = sem("spread_ready")
        span_ready = sem("span_ready")
        span_taken = sem("span_taken")
        steps_ready = sem("steps_ready")
        sum_ready = sem("sum_ready")
        plan_ready = sem("plan_ready")
        plan_in = sem("plan_in")
        x_in = [sem(f"x_in{i}") for i in range(2)]
        xt_done = sem("xt_done")
        ht_copied = sem("ht_copied")
        r_ready = sem("r_ready")
        r_taken = sem("r_taken")
        y_ready = sem("y_ready")
        y_taken = sem("y_taken")
        y_stored = [sem(f"y_stored{i}") for i in range(2)]
        slots_free = sem("slots_free")
        rows_ready = sem("rows_ready")
        gathered = [sem(f"gathered{i}") for i in range(SLOTS)]
        arrived = sem("arrived")
        hot_ready = sem("hot_ready")
        acc_ready = sem("acc_ready")
        acc_taken = sem("acc_taken")
        sig_done = sem("sig_done")
        res_in = sem("res_in")
        stats_done = sem("stats_done")      
        std_done = sem("std_done")
        o_ready = sem("o_ready")
        norm_step = sem("norm_step")
        z_ready = sem("z_ready")
        h_ready = sem("h_ready")
        sum_done = sem("sum_done")
        bias_ready = sem("bias_ready")
        bias_taken = sem("bias_taken")
        res_done = sem("res_done")
        bn_done = sem("bn_done")
        o_stored = sem("o_stored")

        block = ctx.enter_context(nc.Block())

        def edge_view(a):
            return a[0:FB * P * P].rearrange("(b p e) -> p b e", p=P, e=P)

        MOST = T * CP // 2

        def planned(eng, t, k, least=0, most=MOST):
            return eng.value_load(plan[0:1, ds(t * PLAN + k, 1)], min_val=least, max_val=most)

        def window(eng, t):
            return planned(eng, t, 0), planned(eng, t, 1, 2), planned(eng, t, 2, 0, C // 2), planned(eng, t, 3)

        def totals(eng):
            end = planned(eng, T, 1, PAIRS)
            return end, end + planned(eng, T, 3)

        def column(c, n=1):
            return ds(nc.s_assert_within(c, 0, CP - n, skip_runtime_bounds_check_because=(
                "a window's steps end at most SLOTS + 6 chunks past its last chunk")), n)

        @block.sync
        def _(sp):
            sp.wait_ge(pads, 1)
            for raw, given in ((src_r, src), (typ_r, edge_type), (dst_r, dst)):
                sp.dma_start(raw[:, 0:FB * P].rearrange("p (b e) -> p b e", e=P),
                             edge_view(given)).then_inc(edges_in, 16)
                sp.dma_start(raw[0:FULL - FB * P, FB * P:(FB + 1) * P],
                             given[FB * P * P:FULL * P].rearrange("(p e) -> p e", e=P)).then_inc(edges_in, 16)
                sp.dma_start(raw[FULL - FB * P:FULL - FB * P + 1, FB * P:FB * P + E - FULL * P],
                             given[FULL * P:E].rearrange("(p e) -> p e", p=1)).then_inc(edges_in, 16)
            sp.dma_start(xin[:, 0, :], x[0:P, :]).then_inc(x_in[0], 16)
            sp.dma_start(w_sb[:, 0, :, :].rearrange("p k (r e) -> p k r e", e=D)[:, 0],
                         weights[0, :, 0:P, :].rearrange("r k e -> k r e")).then_inc(w0_in, 16)
            sp.dma_start(w_sb[:, 0, :, :].rearrange("p k (r e) -> p k r e", e=D)[:, 1],
                         weights[0, :, P:D, :].rearrange("r k e -> k r e")).then_inc(w0_in, 16)
            for l in range(L):
                sp.dma_start(root_sb[:, l, :, :], roots[l].rearrange("(k p) e -> p k e", p=P)).then_inc(w0_in, 16)
            sp.dma_start(bias_sb[:, :], biases.rearrange("(a l) e -> a (l e)", a=1)).then_inc(w0_in, 16)
            sp.dma_start(xin[:, 1, :], x[P:2 * P, :]).then_inc(x_in[1], 16)
            with sp.Fori(2, T - 2, 2) as t:
                for i in range(2):
                    sp.wait_ge(xt_done, t + i - 1)
                    sp.dma_start(xin[:, i, :], x[ds((t + i) * P, P), :]).then_inc(x_in[i], 16)
            sp.wait_ge(xt_done, T - 2)
            sp.dma_start(xin[0:LAST, 0, :], x[(T - 1) * P:N, :]).then_inc(x_in[0], 16)
            sp.wait_ge(plan_ready, 1)
            sp.dma_start(plan[0:1, :].rearrange("a (t k) -> a t k", k=PLAN), plan_c[0:T + 1, :]).then_inc(plan_in, 16)
            for l in range(1, L):
                for k in range(KD):
                    sp.dma_start(w_sb[:, l, k, :].rearrange("p (r e) -> p r e", e=D),
                                 weights[l, :, k * P:(k + 1) * P, :].rearrange("r k e -> k r e")).then_inc(late_in, 16)
            sp.wait_ge(plan_in, 16)
            total, _ = totals(sp)
            for l in range(L):
                with sp.Fori(0, total, PAIRS) as s:
                    landed = sp.snap((total * l + s) * (16 // PAIRS) + 16)
                    for i in range(SLOTS):
                        sp.wait_ge(gathered[i], landed)
                        if i % 2:
                            sp.sem_inc(arrived, 1)

        @block.gpsimd
        def _(pool):
            pool.iota(part_no[:, :], [[0, 1]], base=0, channel_multiplier=1,
                      allow_small_or_imprecise_dtypes=True).then_inc(consts_pool, 1)
            pool.iota(node_no[:, :], [[1, T * P]], base=0, channel_multiplier=0,
                      allow_small_or_imprecise_dtypes=True).then_inc(consts_pool, 1)
            pool.iota(chunk_no, [[1, CP]], base=1, channel_multiplier=0,
                      allow_small_or_imprecise_dtypes=True).then_inc(consts_pool, 1)
            pool.wait_ge(plan_in, 16)
            total, _ = totals(pool)
            for l in range(L):
                pool.wait_ge(y_stored[0], 16 * T * (l + 1))
                pool.wait_ge(y_stored[1], 16 * T * (l + 1))
                with pool.Fori(0, total, PAIRS) as s:
                    quads = pool.snap((total * l + s) >> 1)
                    for i in range(SLOTS):
                        if i % 4 == 0:
                            pool.wait_ge(rows_ready, quads + (i // 4 + 1))
                            pool.nop(nofuse=True)
                        pool.indirect_dma_start(
                            out=gath[:, i, :], out_offset=None, in_=yrow[l % 2],
                            in_offset=bass.IndirectOffsetOnAxis(ap=rowslot[:, i:i + 1], axis=0),
                        ).then_inc(gathered[i], 16)

        @block.scalar
        def _(act):
            def h_t_copy(n, i, again=True):
                act.wait_ge(xt_done, n + 1)
                if again:
                    act.wait_ge(y_ready, (n - 1) * YG)
                nc.scalar.copy(h_t[:, i, :, :].rearrange("p k m -> p (k m)"),
                               ps_t[i][:, 0:D]).then_inc(ht_copied, 1)

            def y_take(n, again=True):
                act.wait_ge(r_ready, n + 1)
                nc.scalar.copy(hroot[:, ds(n, 1), :], ps_r[:, 0:D]).then_inc(r_taken, 1)
                for half in range(2):
                    if again:
                        act.wait_ge(y_stored[half], n * 16)
                    for k in range(half * HG, (half + 1) * HG):
                        act.wait_ge(y_ready, n * YG + (k + 1))
                        nc.scalar.copy(ystage[:, k * COLS:(k + 1) * COLS], ps_y[k][:, :]).then_inc(y_taken, 1)
                    y_store(n, n, half, ytab[0])

            def y_store(n, t, half, table):
                act.wait_ge(y_taken, n * YG + (half + 1) * HG)
                w = HG * COLS
                act.dma_start(table[ds(t * P, P), half * w:(half + 1) * w],
                              ystage[:, half * w:(half + 1) * w]).then_inc(y_stored[half], 16)

            h_t_copy(0, 0, False)
            h_t_copy(1, 1, False)
            y_take(0, False)
            with act.Fori(1, T - 3, 2) as t:
                h_t_copy(t + 1, 0)
                y_take(t)
                h_t_copy(t + 2, 1)
                y_take(t + 1)
            h_t_copy(T - 1, 0)
            for t in (T - 2, T - 1):
                y_take(t)

            act.wait_ge(plan_in, 16)
            _, steps = totals(act)

            def name_rows(l, t):
                first, end, chunk, twice = window(act, t)
                new = planned(act, t, 4)
                used = act.snap(steps * l + twice + 2)
                with act.Fori(new, end, 2) as g:
                    act.wait_ge(slots_free, g + used)
                    nc.scalar.copy(rowslot[:, ds((g & (PAIRS - 2)) * 2, 4)],
                                   rows_t[:, column((chunk + (g - first)) * 2, 4)]).then_inc(rows_ready, 1)

            for l in range(L - 1):
                def store_both(t):
                    for half in range(2):
                        y_store((l + 1) * T + t, t, half, ytab[(l + 1) % 2])

                name_rows(l, 0)
                name_rows(l, 1)
                with act.Fori(2, T) as t:
                    name_rows(l, t)
                    store_both(t - 2)
                store_both(T - 2)
                store_both(T - 1)

            def last_steps(t):
                def at(lag):
                    return not isinstance(t, int) or 0 <= t - lag < T

                if at(1):
                    rows = LAST if isinstance(t, int) and t - 1 == T - 1 else P
                    if not isinstance(t, int) or t >= 2:
                        act.wait_ge(stats_done, t - 1)
                    act.dma_start(xin[0:rows, 0, :], x[ds((t - 1) * P, rows), :]).then_inc(res_in, 16)
                    act.wait_ge(sum_done, t)
                    nc.scalar.activation(hroot[:, ds(t - 1, 1), :], hroot[:, ds(t - 1, 1), :],
                                         ACT.Sigmoid).then_inc(sig_done, 1)
                if at(2):
                    act.wait_ge(stats_done, t - 1)
                    nc.scalar.activation(std[:, :], mv[:, 1:2], ACT.Sqrt, bias=eps[:, 0:1]).then_inc(std_done, 1)
                if at(3):
                    rows = LAST if isinstance(t, int) and t - 3 == T - 1 else P
                    act.wait_ge(o_ready, t - 2)
                    act.dma_start(out[ds((t - 3) * P, rows), :], o_sb[0:rows, :]).then_inc(o_stored, 16)

            for t in range(4):
                name_rows(L - 1, t)
                last_steps(t)
            with act.Fori(4, T) as t:
                name_rows(L - 1, t)
                last_steps(t)
            for t in range(T, T + 3):
                last_steps(t)
            act.wait_ge(o_stored, 16 * T)

        @block.vector
        def _(dve):
            chain = [0]

            def link(made):
                chain[0] += 1
                made.then_inc(dve_step, 1)
                dve.wait_ge(dve_step, chain[0])

            V = nc.vector
            V.memset(src_r[:, FB * P:CP], 0)
            V.memset(typ_r[:, FB * P:CP], 0)
            V.memset(rowslot[:, :], 0)
            V.memset(ones[:, :], 1.0)
            V.memset(nought[:, :], 0.0)
            V.memset(plan_c[:, :], 0)
            V.memset(eps[:, :], EPS)
            link(V.memset(dst_r[:, FB * P:CP], int(NO_NODE)))
            dve.sem_inc(pads, 1)
            dve.wait_ge(consts_pool, 3)
            V.tensor_scalar(ident[:, :], node_no[:, 0:P], part_no[:, 0:1], None, ALU.is_equal)
            V.tensor_scalar(tri[:, :], node_no[:, 0:P], part_no[:, 0:1], None, ALU.is_ge)
            V.tensor_scalar(lo[:, :], part_no[:, :], float(P), None, ALU.mult)
            V.tensor_scalar(hi[:, :], part_no[:, :], float(P), float(P), ALU.mult, ALU.add)
            V.tensor_scalar(v["is_window"][:, :], part_no[:, :], float(T), None, ALU.is_lt)
            V.tensor_scalar(v["is_last"][:, :], part_no[:, :], float(T - 1), None, ALU.is_ge)
            link(V.tensor_scalar(part_1[:, :], part_no[:, :], 1.0, None, ALU.add))
            V.tensor_scalar(shift[:, :], node_no[:, 0:P], part_1[:, 0:1], None, ALU.is_equal)
            dve.wait_ge(edges_in, 9 * 16)
            V.scalar_tensor_tensor(rows_f, src_r[:, :], float(R), typ_r[:, :], ALU.mult, ALU.add)
            link(V.tensor_copy(dst_f, dst_r[:, :]))
            dve.sem_inc(edge_rows, 1)
            link(V.scalar_tensor_tensor(dst_v, dst_f, NO_NODE / 2, dst_f, ALU.is_lt, ALU.mult))
            by_chunk = "p (b e) -> p b e"
            V.tensor_reduce(dlow[:, :], dst_f.rearrange(by_chunk, e=P), AXX, ALU.min)
            link(V.tensor_reduce(dhigh[:, :], dst_v.rearrange(by_chunk, e=P), AXX, ALU.max))
            for end, made in ((dlow, spread), (dhigh, spread_hi)):
                V.tensor_tensor(made.rearrange(by_chunk, e=P), ident[:, :].unsqueeze(1).broadcast_to([P, CB, P]),
                                end[:, :].unsqueeze(2).broadcast_to([P, CB, P]), ALU.mult).then_inc(spread_ready, 1)
            for i, to in enumerate((rows_t, dst_t)):
                for b in range(4):
                    dve.wait_ge(tr_ready, 4 * i + b + 1)
                    w = min(COLS, CP - b * COLS)
                    V.tensor_copy(to[:, b * COLS:b * COLS + w], bank[4 * i + b][:, 0:w]).then_inc(tr_taken, 1)
            for b in range(4):
                dve.wait_ge(span_ready, b + 1)
                w = min(COLS, CP - b * COLS)
                V.tensor_scalar(reach_lo[:, b * COLS:b * COLS + w], bank[b][:, 0:w], hi[:, 0:1], None,
                                ALU.is_lt).then_inc(span_taken, 1)
            dve.wait_ge(span_taken, 4)
            for b in range(4):
                dve.wait_ge(span_ready, b + 5)
                w = min(COLS, CP - b * COLS)
                V.scalar_tensor_tensor(reach[:, b * COLS:b * COLS + w], bank[4 + b][:, 0:w], lo[:, 0:1],
                                       reach_lo[:, b * COLS:b * COLS + w], ALU.is_ge, ALU.mult).then_inc(span_taken, 1)
            dve.wait_ge(span_taken, 8)
            link(V.tensor_tensor(reach_lo, reach, chunk_no, ALU.mult))
            link(V.tensor_reduce(v["last_1"][:, :], reach_lo, AXX, ALU.max))
            link(V.tensor_scalar(spread, chunk_no, -1.0, FAR + 1, ALU.mult, ALU.add))
            link(V.tensor_tensor(reach_lo, reach, spread, ALU.mult))
            link(V.tensor_reduce(v["from_end"][:, :], reach_lo, AXX, ALU.max))
            link(V.tensor_scalar(v["first_far"][:, :], v["from_end"][:, :], -1.0, FAR, ALU.mult, ALU.add))
            link(V.tensor_scalar(v["first"][:, :], v["first_far"][:, :], float(C - 1), None, ALU.min))
            link(V.scalar_tensor_tensor(v["last"][:, :], v["last_1"][:, :], -1.0, v["first"][:, :], ALU.add, ALU.max))
            V.tensor_copy(vi["i0"][:, :], v["first"][:, :])
            link(V.tensor_copy(vi["i1"][:, :], v["last"][:, :]))
            V.tensor_scalar(vi["i2"][:, :], vi["i0"][:, :], 2, None, ALU.arith_shift_right)
            link(V.tensor_scalar(vi["i3"][:, :], vi["i1"][:, :], 2, None, ALU.arith_shift_right))
            V.tensor_copy(v["end"][:, :], vi["i3"][:, :])
            link(V.tensor_copy(v["first_quad"][:, :], vi["i2"][:, :]))
            link(V.scalar_tensor_tensor(v["last_quad"][:, :], v["first_quad"][:, :], 1.0, v["end"][:, :], ALU.add, ALU.max))
            link(V.tensor_scalar(next_quad[:, :], v["last_quad"][:, :], 1.0, None, ALU.add))
            dve.sem_inc(steps_ready, 1)
            link(V.tensor_tensor(v["many"][:, :], next_quad[:, :], v["first_quad"][:, :], ALU.subtract))
            link(V.tensor_tensor(v["quads"][:, :], v["many"][:, :], v["is_window"][:, :], ALU.mult))
            dve.wait_ge(sum_ready, 1)
            link(V.scalar_tensor_tensor(v["same"][:, :], v["first_quad"][:, :], 1.0, acc[:, 0:1], ALU.add, ALU.is_equal))
            link(V.scalar_tensor_tensor(counts[:, 1:2], v["quads"][:, :], 2.0, v["same"][:, :], ALU.is_ge, ALU.mult))
            link(V.tensor_tensor(counts[:, 0:1], v["quads"][:, :], counts[:, 1:2], ALU.subtract))
            dve.sem_inc(steps_ready, 1)
            dve.wait_ge(sum_ready, 2)
            V.tensor_scalar(v["end"][:, :], acc[:, 2:3], 2.0, None, ALU.mult)
            V.tensor_scalar(plan_c[:, 3:4], acc[:, 3:4], 2.0, None, ALU.mult)
            V.tensor_scalar(v["twice"][:, :], counts[:, 0:1], 2.0, None, ALU.mult)
            link(V.tensor_scalar(v["share"][:, :], counts[:, 1:2], 2.0, None, ALU.mult))
            link(V.tensor_tensor(v["start"][:, :], v["end"][:, :], v["twice"][:, :], ALU.subtract))
            V.tensor_copy(plan_c[:, 4:5], v["start"][:, :])
            V.tensor_tensor(plan_c[:, 0:1], v["start"][:, :], v["share"][:, :], ALU.subtract)
            V.tensor_scalar(plan_c[:, 2:3], v["first_quad"][:, :], 2.0, None, ALU.mult)
            link(V.tensor_scalar(vi["i4"][:, :], v["end"][:, :], float(PAIRS - 1), None, ALU.add))
            link(V.tensor_scalar(vi["i5"][:, :], vi["i4"][:, :], LOG_PAIRS, LOG_PAIRS, ALU.arith_shift_right, ALU.arith_shift_left))
            link(V.tensor_tensor(v["end_up"][:, :], vi["i5"][:, :], v["end"][:, :], ALU.subtract))
            link(V.tensor_tensor(v["many"][:, :], v["end_up"][:, :], v["is_last"][:, :], ALU.mult))
            link(V.tensor_tensor(plan_c[:, 1:2], v["many"][:, :], v["end"][:, :], ALU.add))
            dve.sem_inc(plan_ready, 1)

            dve.wait_ge(plan_in, 16)
            _, steps = totals(dve)

            def one_hots(l, t, between=None):
                first, end, chunk, twice = window(dve, t)
                used = dve.snap(steps * l + twice + (PAIRS - 1))
                nodes = dve.snap(t * P)
                second = dve.snap(first + 2)

                def quad(g):
                    c = dve.snap((chunk + (g - first)) * 2)
                    wanted = [dve.snap(g + used + j) for j in range(2)]
                    of = [c, dve.snap(c + 2)]
                    for j in range(2):
                        dve.wait_ge(slots_free, wanted[j])
                        V.tensor_tensor(hot[:, 2 * j:2 * j + 2, :],
                                        node_no[:, ds(nodes, P)].unsqueeze(1).broadcast_to([P, 2, P]),
                                        dst_t[:, column(of[j], 2)].unsqueeze(2).broadcast_to([P, 2, P]),
                                        ALU.is_equal).then_inc(hot_ready, 1)

                if between:
                    between[0]()
                quad(first)
                if between:
                    between[1]()
                with dve.Fori(second, end, 2) as g:
                    quad(g)

            def flat(ap):
                return ap.rearrange("p a d -> p (a d)")

            def layer_sum(l, t, to):
                dve.wait_ge(acc_ready, l * T + t + 1)
                V.tensor_tensor(s_sb[:, :], acc[:, 0:D], flat(hroot[:, ds(t, 1), :]), ALU.add).then_inc(acc_taken, 1)
                dve.wait_ge(acc_taken, l * T + t + 1)
                return V.tensor_tensor(to, s_sb[:, :], bias_all[:, l, :], ALU.add)

            def next_h(l, t):
                layer_sum(l, t, z_sb[:, :]).then_inc(z_ready, 1)
                dve.wait_ge(z_ready, l * T + t + 1)
                V.tensor_scalar(h_sb[:, :], z_sb[:, :], 0.0, None, ALU.max).then_inc(h_ready, 1)

            def empty_products(n, t):
                dve.wait_ge(r_ready, n + 1)
                V.tensor_copy(flat(hroot[:, ds(t, 1), :]), ps_r[:, 0:D]).then_inc(r_taken, 1)
                for half in range(2):
                    dve.wait_ge(y_stored[half], n * 16)
                    for k in range(half * HG, (half + 1) * HG):
                        dve.wait_ge(y_ready, n * YG + (k + 1))
                        V.tensor_copy(ystage[:, k * COLS:(k + 1) * COLS], ps_y[k][:, :]).then_inc(y_taken, 1)

            def h_t_copy(n):
                dve.wait_ge(xt_done, n + 1)
                V.tensor_copy(h_t[:, 0, :, :].rearrange("p k m -> p (k m)"), ps_t[0][:, 0:D]).then_inc(ht_copied, 1)

            dve.wait_ge(bias_ready, 1)
            V.tensor_copy(bias_all[:, 0, :], bank[0][:, 0:D])
            V.tensor_copy(bias_all[:, 1, :], bank[0][:, D:2 * D])
            V.tensor_copy(bias_all[:, 2, :], ps_t[1][:, 0:D]).then_inc(bias_taken, 1)
            for l in range(L - 1):
                def n(t):
                    return (l + 1) * T + t

                def after_products(t, lag):
                    if lag:
                        empty_products(n(t) - 1, t - 1)
                    h_t_copy(n(t))

                one_hots(l, 0)
                one_hots(l, 1, (lambda: next_h(l, 0), lambda: after_products(0, False)))
                with dve.Fori(2, T) as t:
                    one_hots(l, t, (lambda: next_h(l, t - 1), lambda: after_products(t - 1, True)))
                next_h(l, T - 1)
                after_products(T - 1, True)
                empty_products(n(T - 1), T - 1)

            def last_steps(t):
                def at(lag):
                    return not isinstance(t, int) or 0 <= t - lag < T

                if at(0):
                    layer_sum(L - 1, t, flat(hroot[:, ds(t, 1), :])).then_inc(sum_done, 1)
                if at(2):
                    dve.wait_ge(std_done, t - 1)
                    if not isinstance(t, int) or t >= 3:
                        dve.wait_ge(o_stored, 16 * (t - 2))
                    V.reciprocal(rstd[:, :], std[:, :]).then_inc(norm_step, 1)
                    dve.wait_ge(norm_step, t - 1)
                    V.tensor_scalar(o_sb[:, :], z_sb[:, :], mv[:, 0:1],
                                    rstd[:, 0:1], ALU.subtract, ALU.mult).then_inc(o_ready, 1)
                if at(1):
                    dve.wait_ge(sig_done, t)
                    dve.wait_ge(res_in, 16 * t)
                    if not isinstance(t, int) or t >= 2:
                        dve.wait_ge(o_ready, t - 1)
                    V.tensor_tensor(z_sb[:, :], hroot[:, ds(t - 1, 1), :].rearrange("p a d -> p (a d)"),
                                    xin[:, 0, :], ALU.add).then_inc(res_done, 1)
                    dve.wait_ge(res_done, t)
                    V.bn_stats(stats[:, :], z_sb[:, :]).then_inc(bn_done, 1)
                    dve.wait_ge(bn_done, t)
                    dve.nop(nofuse=True)
                    V.bn_aggr(mv[:, :], stats[:, :]).then_inc(stats_done, 1)

            for t in range(3):
                one_hots(L - 1, t)
                last_steps(t)
            with dve.Fori(3, T) as t:
                one_hots(L - 1, t)
                last_steps(t)
            for t in range(T, T + 2):
                last_steps(t)

        @block.tensor
        def _(pe):
            mm = nc.tensor.matmul
            pe.sem_inc(slots_free, PAIRS)
            pe.wait_ge(edge_rows, 1)
            for i, given in enumerate((rows_f, dst_f)):
                for b in range(CB):
                    made = nc.tensor.transpose(bank[4 * i + b // 4][:, (b % 4) * P:(b % 4 + 1) * P],
                                               given[:, b * P:(b + 1) * P], ident[:, :])
                    if b % 4 == 3 or b == CB - 1:
                        made.then_inc(tr_ready, 1)
            pe.wait_ge(tr_taken, 8)
            for i, given in enumerate((spread, spread_hi)):
                pe.wait_ge(spread_ready, i + 1)
                for b in range(4):
                    w = min(COLS, CP - b * COLS)
                    mm(bank[4 * i + b][:, 0:w], lhsT=ones[:, :], rhs=given[:, b * COLS:b * COLS + w],
                       start=True, stop=True).then_inc(span_ready, 1)
            pe.wait_ge(span_taken, 8)
            pe.wait_ge(w0_in, 16 * (KD + L + 1))

            def transposed(given, i):
                for k in range(KD):
                    made = nc.tensor.transpose(ps_t[i][:, k * P:(k + 1) * P], given[:, k * P:(k + 1) * P], ident[:, :])
                made.then_inc(xt_done, 1)

            def x_tile(n, i, again=True):
                pe.wait_ge(x_in[i], 8 * (n - i) + 16)
                if again:
                    pe.wait_ge(ht_copied, n - 1)
                transposed(xin[:, i, :], i)

            def products(n, i, l, again=True):
                pe.wait_ge(ht_copied, n + 1)
                if again:
                    pe.wait_ge(r_taken, n)
                for k in range(KD):
                    made = mm(ps_r[:, 0:D], lhsT=h_t[:, i, k, :], rhs=root_sb[:, l, k, :],
                              start=(k == 0), stop=(k == KD - 1))
                made.then_inc(r_ready, 1)
                for g in range(YG):
                    if again:
                        pe.wait_ge(y_taken, n * YG + (g + 1 - YG))
                    for k in range(KD):
                        made = mm(ps_y[g][:, :], lhsT=h_t[:, i, k, :], rhs=w_sb[:, l, k, g * COLS:(g + 1) * COLS],
                                  start=(k == 0), stop=(k == KD - 1))
                    made.then_inc(y_ready, 1)

            x_tile(0, 0, False)
            x_tile(1, 1, False)
            products(0, 0, 0, False)
            pe.wait_ge(steps_ready, 1)
            mm(acc[:, 0:1], lhsT=shift[:, :], rhs=next_quad[:, :], start=True, stop=True).then_inc(sum_ready, 1)
            x_tile(2, 0)
            products(1, 1, 0)
            x_tile(3, 1)
            products(2, 0, 0)
            pe.wait_ge(steps_ready, 2)
            mm(acc[:, 2:4], lhsT=tri[:, :], rhs=counts[:, :], start=True, stop=True).then_inc(sum_ready, 1)
            with pe.Fori(3, T - 3, 2) as t:
                x_tile(t + 1, 0)
                products(t, 1, 0)
                x_tile(t + 2, 1)
                products(t + 1, 0, 0)
            x_tile(T - 1, 0)
            products(T - 2, 1, 0)
            products(T - 1, 0, 0)

            pe.wait_ge(plan_in, 16)
            mm(bank[0][:, 0:2 * D], lhsT=ones[0:1, :], rhs=bias_sb[0:1, 0:2 * D], start=True, stop=True)
            mm(ps_t[1][:, 0:D], lhsT=ones[0:1, :], rhs=bias_sb[0:1, 2 * D:3 * D],
               start=True, stop=True).then_inc(bias_ready, 1)
            pe.wait_ge(bias_taken, 1)
            total, steps = totals(pe)

            def add_steps(l, t, meanwhile=None):
                if meanwhile:
                    meanwhile()
                first, end, twice = planned(pe, t, 0), planned(pe, t, 1, 2), planned(pe, t, 3)
                step = pe.snap(steps * l + twice)
                before = pe.snap(total * l + 2)
                mm(acc[:, 0:D], lhsT=nought[0:1, 0:P], rhs=nought[0:1, :], start=True, stop=False)
                with pe.Fori(first, end, 2) as g:
                    at = pe.snap((g & (PAIRS - 2)) * (2 * D))
                    of = [at] + [pe.snap(at + i * D) for i in range(1, 4)]
                    wanted = [pe.snap(g + step + (j + 1)) for j in range(2)]
                    pe.wait_ge(arrived, g + before)
                    for i in range(4):
                        if i % 2 == 0:
                            pe.wait_ge(hot_ready, wanted[i // 2])
                        made = mm(acc[:, 0:D], lhsT=hot[:, i, :], rhs=gath_flat[:, ds(of[i], D)],
                                  start=False, stop=False)
                        if i % 2:
                            made.then_inc(slots_free, 1)
                mm(acc[:, 0:D], lhsT=nought[0:1, 0:P], rhs=nought[0:1, :], start=False, stop=True).then_inc(acc_ready, 1)

            def transpose_h(l, t):
                pe.wait_ge(h_ready, l * T + t + 1)
                transposed(h_sb, 0)

            for l in range(L - 1):
                def n(t):
                    return (l + 1) * T + t

                def between(t):
                    products(n(t) - 1, 0, l + 1)
                    transpose_h(l, t)

                add_steps(l, 0)
                if l == 0:
                    pe.wait_ge(late_in, 16 * (L - 1) * KD)
                add_steps(l, 1, lambda: transpose_h(l, 0))
                with pe.Fori(2, T) as t:
                    add_steps(l, t, lambda: between(t - 1))
                between(T - 1)
                products(n(T - 1), 0, l + 1)
            add_steps(L - 1, 0)
            with pe.Fori(1, T) as t:
                pe.wait_ge(acc_taken, (L - 1) * T + t)
                add_steps(L - 1, t)


_INS = ['x', 'src', 'dst', 'edge_type_8', 'L0_gnn_weights', 'L0_gnn_roots', 'L0_gnn_biases']


def kernel(**inputs):
    import numpy as _np
    import concourse.bacc as _bacc
    from concourse import mybir as _mybir
    from concourse.bass_utils import run_bass_kernel_spmd as _run

    nc = _bacc.Bacc("TRN2", target_bir_lowering=False, num_devices=1)
    arrays, args = {}, []
    for name in _INS:
        a = _np.ascontiguousarray(inputs[name])
        arrays[f"in_{name}"] = a
        args.append(nc.dram_tensor(f"in_{name}", a.shape, _mybir.dt.from_np(a.dtype), kind="ExternalInput").ap())
    out = nc.dram_tensor("out_0", inputs['x'].shape, _mybir.dt.float32, kind="ExternalOutput").ap()
    relational_graph_layers(nc, *args, out)
    r = _run(nc, [arrays], core_ids=[0])
    return r.results[0]["out_0"]
```

```python
import concourse.bass as bass
from concourse import mybir
from contextlib import ExitStack

F32 = mybir.dt.float32
I32 = mybir.dt.int32
ALU = mybir.AluOpType
ACT = mybir.ActivationFunctionType
AXX = mybir.AxisListType.X
ds = bass.ds

P = 128
SLOTS = 32
PAIRS = SLOTS // 2
LOG_PAIRS = PAIRS.bit_length() - 1
PLAN = 8
COLS = 512
NO_NODE = float(1 << 20)
FAR = 2048.0


def relational_graph_layers(nc, x, src, dst, edge_type, weights, roots, biases, out):
    N, D = x.shape
    E = src.shape[0]
    L, R = weights.shape[0], weights.shape[1]
    T = -(-N // P)
    LAST = N - (T - 1) * P
    C = -(-E // P)
    CB = -(-(C + SLOTS + 7) // P)
    CP = CB * P
    FULL = E // P
    FB = FULL // P
    KD = D // P
    RD = R * D
    YG = RD // COLS
    HG = YG // 2
    LATE = T - 1 - 2 * (L - 1) * R
    ROOTS = (0, T * 5 // 24 * 2, T * 3 // 8 * 2, T)
    EPS = 1e-5

    ctx = ExitStack()
    with ctx:
        def sb(name, shape, dt=F32):
            return ctx.enter_context(nc.sbuf_tensor(name, shape, dt))

        def sem(name):
            return ctx.enter_context(nc.semaphore(name))

        ytab = [nc.dram_tensor(f"ytab{i}", (T * P, RD), F32).ap() for i in range(2)]
        weight_rows = weights.rearrange("l r k e -> (l r k) e")
        yrow = [y.rearrange("n (r e) -> (n r) e", e=D) for y in ytab]

        w_sb = sb("w_sb", [P, L, KD, RD])
        root_sb = sb("root_sb", [P, L, KD, D])
        bias_sb = sb("bias_sb", [1, L * D])
        hroot = sb("hroot", [P, T, D])
        rows_t = sb("rows_t", [P, CP], I32)
        dst_t = sb("dst_t", [P, CP])
        node_no = sb("node_no", [P, T * P])
        ident = sb("ident", [P, P])
        ones = sb("ones", [P, P])
        nought = sb("nought", [1, D], mybir.dt.bfloat16)
        bias_all = sb("bias_all", [P, L, D])
        eps = sb("eps", [P, 1])
        plan = sb("plan", [1, (T + 1) * PLAN], I32)
        gath = sb("gath", [P, SLOTS, D])
        gath_flat = gath[:, :, :].rearrange("p s d -> p (s d)")
        rowslot = sb("rowslot", [P, SLOTS], I32)
        hot = sb("hot", [P, 4, P])
        xin = sb("xin", [P, 2, D])
        h_sb = sb("h_sb", [P, D])
        s_sb = sb("s_sb", [P, D])
        h_t = sb("h_t", [P, 2, KD, P])
        ystage = sb("ystage", [P, RD])
        stats = sb("stats", [P, 6])
        mv = sb("mv", [P, 2])
        std = sb("std", [P, 1])
        rstd = sb("rstd", [P, 1])
        z_sb = sb("z_sb", [P, D])
        o_sb = sb("o_sb", [P, D])
        late = w_sb[:, 1:L, :, :].rearrange("p l k n -> p (l k n)")
        rows_f = late[:, 0:CP]
        dst_f = late[:, CP:2 * CP]
        dst_v = late[:, 2 * CP:3 * CP]
        spread_hi = dst_v
        reach_lo = rows_f
        reach = dst_f
        spread = late[:, 3 * CP:4 * CP]
        chunk_no = gath_flat[:, 0:CP]
        src_r, typ_r, dst_r = (gath_flat[:, i * CP:(i + 1) * CP].bitcast(I32) for i in range(1, 4))
        part_no = sb("part_no", [P, 1])
        lo = sb("lo", [P, 1])
        hi = sb("hi", [P, 1])
        dlow = sb("dlow", [P, CB])
        dhigh = sb("dhigh", [P, CB])
        tri = sb("tri", [P, P])
        shift = sb("shift", [P, P])
        v = {name: sb(name, [P, 1]) for name in (
            "last_1", "from_end", "first_far", "first", "last", "is_window", "is_last", "first_quad",
            "last_quad", "quads", "same", "many", "share", "end", "end_up", "start", "twice")}
        vi = {name: sb(name, [P, 1], I32) for name in ("i0", "i1", "i2", "i3", "i4", "i5")}
        part_1 = sb("part_1", [P, 1])
        next_quad = sb("next_quad", [P, 1])
        counts = sb("counts", [P, 2])
        plan_c = sb("plan_c", [P, PLAN], I32)

        bank = [ctx.enter_context(nc.psum_tensor(f"bank{i}", [P, COLS], F32)) for i in range(8)]
        acc = bank[0]
        ps_t = [bank[1], bank[7]]
        ps_r = bank[2]
        ps_y = bank[3:3 + YG]
        ps_root = [ps_r, ps_y[0]]

        consts_pool = sem("consts_pool")
        pads = sem("pads")
        edges_in = sem("edges_in")
        w0_in = sem("w0_in")
        ident_ready = sem("ident_ready")
        bias_in = sem("bias_in")
        late_in = sem("late_in")
        dve_step = sem("dve_step")
        edge_rows = sem("edge_rows")
        tr_ready = sem("tr_ready")
        tr_taken = sem("tr_taken")
        spread_ready = sem("spread_ready")
        span_ready = sem("span_ready")
        span_taken = sem("span_taken")
        steps_ready = sem("steps_ready")
        sum_ready = sem("sum_ready")
        plan_ready = sem("plan_ready")
        plan_in = sem("plan_in")
        x_in = [sem(f"x_in{i}") for i in range(2)]
        xt_done = sem("xt_done")
        ht_copied = sem("ht_copied")
        xt_saved = sem("xt_saved")
        root_in = sem("root_in")
        r_ready = sem("r_ready")
        r_taken = sem("r_taken")
        y_ready = sem("y_ready")
        y_taken = sem("y_taken")
        y_stored = [sem(f"y_stored{i}") for i in range(2)]
        slots_free = sem("slots_free")
        rows_ready = sem("rows_ready")
        gathered = [sem(f"gathered{i}") for i in range(SLOTS)]
        arrived = sem("arrived")
        hot_ready = sem("hot_ready")
        acc_ready = sem("acc_ready")
        acc_taken = sem("acc_taken")
        sig_done = sem("sig_done")
        res_in = sem("res_in")
        stats_done = sem("stats_done")
        std_done = sem("std_done")
        o_ready = sem("o_ready")
        norm_step = sem("norm_step")
        z_ready = sem("z_ready")
        h_ready = sem("h_ready")
        sum_done = sem("sum_done")
        bias_ready = sem("bias_ready")
        bias_taken = sem("bias_taken")
        res_done = sem("res_done")
        bn_done = sem("bn_done")
        o_stored = sem("o_stored")

        block = ctx.enter_context(nc.Block())

        def edge_view(a):
            return a[0:FB * P * P].rearrange("(b p e) -> p b e", p=P, e=P)

        MOST = T * CP // 2

        def planned(eng, t, k, least=0, most=MOST):
            return eng.value_load(plan[0:1, ds(t * PLAN + k, 1)], min_val=least, max_val=most)

        def window(eng, t):
            return planned(eng, t, 0), planned(eng, t, 1, 2), planned(eng, t, 2, 0, C // 2), planned(eng, t, 3)

        def totals(eng):
            end = planned(eng, T, 1, PAIRS)
            return end, end + planned(eng, T, 3)

        def column(c, n=1):
            return ds(nc.s_assert_within(c, 0, CP - n, skip_runtime_bounds_check_because=(
                "a window's steps end at most SLOTS + 6 chunks past its last chunk")), n)

        @block.sync
        def _(sp):
            sp.dma_start(xin[:, 0, :], x[0:P, :]).then_inc(x_in[0], 16)
            for k in range(KD):
                sp.dma_start(w_sb[:, 0, k, :].rearrange("p (r e) -> p r e", e=D),
                             weights[0, :, k * P:(k + 1) * P, :].rearrange("r k e -> k r e")).then_inc(w0_in, 16)
            sp.dma_start(root_sb[:, 0, :, :], roots[0].rearrange("(k p) e -> p k e", p=P)).then_inc(w0_in, 16)
            sp.wait_ge(pads, 1)
            for raw, given in ((src_r, src), (typ_r, edge_type), (dst_r, dst)):
                sp.dma_start(raw[:, 0:FB * P].rearrange("p (b e) -> p b e", e=P),
                             edge_view(given)).then_inc(edges_in, 16)
                sp.dma_start(raw[0:FULL - FB * P, FB * P:(FB + 1) * P],
                             given[FB * P * P:FULL * P].rearrange("(p e) -> p e", e=P)).then_inc(edges_in, 16)
                sp.dma_start(raw[FULL - FB * P:FULL - FB * P + 1, FB * P:FB * P + E - FULL * P],
                             given[FULL * P:E].rearrange("(p e) -> p e", p=1)).then_inc(edges_in, 16)
            sp.dma_start(bias_sb[:, :], biases.rearrange("(a l) e -> a (l e)", a=1)).then_inc(bias_in, 16)
            sp.dma_start(xin[:, 1, :], x[P:2 * P, :]).then_inc(x_in[1], 16)

            def load_x(t, i):
                sp.wait_ge(xt_done, t + i - 1)
                sp.dma_start(xin[:, i, :], x[ds((t + i) * P, P), :]).then_inc(x_in[i], 16)

            with sp.Fori(2, LATE, 2) as t:
                for i in range(2):
                    load_x(t, i)
            sp.wait_ge(plan_ready, 1)
            sp.dma_start(plan[0:1, :].rearrange("a (t k) -> a t k", k=PLAN), plan_c[0:T + 1, :]).then_inc(plan_in, 16)
            for l in range(1, L):
                sp.dma_start(root_sb[:, l, :, :], roots[l].rearrange("(k p) e -> p k e", p=P)).then_inc(late_in, 16)
            for l in range(1, L):
                begin = LATE + (l - 1) * 2 * R
                with sp.Fori(begin, begin + 2 * R - 1, 2) as t:
                    for i in range(2):
                        load_x(t, i)
                        r_cols = sp.snap((t - begin) * (D // 2))
                        sp.dma_start(w_sb[:, l, i, ds(r_cols, D)],
                                     weight_rows[ds(r_cols + (l * R * D + i * P), P), :]).then_inc(late_in, 16)
            sp.wait_ge(xt_done, T - 2)
            sp.dma_start(xin[0:LAST, 0, :], x[(T - 1) * P:N, :]).then_inc(x_in[0], 16)
            sp.wait_ge(plan_in, 16)
            total, _ = totals(sp)
            for l in range(L):
                with sp.Fori(0, total, PAIRS) as s:
                    landed = sp.snap((total * l + s) * (16 // PAIRS) + 16)
                    for i in range(SLOTS):
                        sp.wait_ge(gathered[i], landed)
                        if i % 2:
                            sp.sem_inc(arrived, 1)

        @block.gpsimd
        def _(pool):
            pool.iota(part_no[:, :], [[0, 1]], base=0, channel_multiplier=1,
                      allow_small_or_imprecise_dtypes=True).then_inc(consts_pool, 1)
            pool.iota(node_no[:, 0:P], [[1, P]], base=0, channel_multiplier=0,
                      allow_small_or_imprecise_dtypes=True).then_inc(consts_pool, 1)
            pool.iota(chunk_no, [[1, CP]], base=1, channel_multiplier=0,
                      allow_small_or_imprecise_dtypes=True).then_inc(consts_pool, 1)
            pool.iota(node_no[:, P:T * P], [[1, (T - 1) * P]], base=P, channel_multiplier=0,
                      allow_small_or_imprecise_dtypes=True).then_inc(consts_pool, 1)
            pool.wait_ge(plan_in, 16)
            total, _ = totals(pool)
            for l in range(L):
                pool.wait_ge(y_stored[0], 16 * T * (l + 1))
                pool.wait_ge(y_stored[1], 16 * T * (l + 1))
                with pool.Fori(0, total, PAIRS) as s:
                    quads = pool.snap((total * l + s) >> 1)
                    for i in range(SLOTS):
                        if i % 4 == 0:
                            pool.wait_ge(rows_ready, quads + (i // 4 + 1))
                            pool.nop(nofuse=True)
                        pool.indirect_dma_start(
                            out=gath[:, i, :], out_offset=None, in_=yrow[l % 2],
                            in_offset=bass.IndirectOffsetOnAxis(ap=rowslot[:, i:i + 1], axis=0),
                        ).then_inc(gathered[i], 16)

        @block.scalar
        def _(act):
            def h_t_copy(n, i, again=True):
                act.wait_ge(xt_done, n + 1)
                if again:
                    act.wait_ge(y_ready, (n - 1) * YG)
                nc.scalar.copy(h_t[:, i, :, :].rearrange("p k m -> p (k m)"),
                               ps_t[i][:, 0:D]).then_inc(ht_copied, 1)
                nc.scalar.copy(hroot[:, ds(n, 1), :].rearrange("p a d -> p (a d)"),
                               ps_t[i][:, 0:D]).then_inc(xt_saved, 1)

            def y_take(n, again=True):
                for half in range(2):
                    if again:
                        act.wait_ge(y_stored[half], n * 16)
                    for k in range(half * HG, (half + 1) * HG):
                        act.wait_ge(y_ready, n * YG + (k + 1))
                        nc.scalar.copy(ystage[:, k * COLS:(k + 1) * COLS], ps_y[k][:, :]).then_inc(y_taken, 1)
                    y_store(n, n, half, ytab[0])

            def y_store(n, t, half, table):
                act.wait_ge(y_taken, n * YG + (half + 1) * HG)
                w = HG * COLS
                act.dma_start(table[ds(t * P, P), half * w:(half + 1) * w],
                              ystage[:, half * w:(half + 1) * w]).then_inc(y_stored[half], 16)

            h_t_copy(0, 0, False)
            y_take(0, False)
            h_t_copy(1, 1, False)
            y_take(1)
            h_t_copy(2, 0)
            with act.Fori(2, T - 3, 2) as t:
                h_t_copy(t + 1, 1)
                y_take(t)
                h_t_copy(t + 2, 0)
                y_take(t + 1)
            h_t_copy(T - 2, 1)
            y_take(T - 3)
            h_t_copy(T - 1, 0)
            y_take(T - 2)

            act.wait_ge(plan_in, 16)
            _, steps = totals(act)

            def name_rows(l, t, after_two=None):
                first, end, chunk, twice = window(act, t)
                new = planned(act, t, 4)
                used = act.snap(steps * l + twice + 2)

                def quad(g):
                    act.wait_ge(slots_free, g + used)
                    nc.scalar.copy(rowslot[:, ds((g & (PAIRS - 2)) * 2, 4)],
                                   rows_t[:, column((chunk + (g - first)) * 2, 4)]).then_inc(rows_ready, 1)

                if after_two:
                    quad(new)
                    quad(act.snap(new + 2))
                    new = act.snap(new + 4)
                    after_two()
                with act.Fori(new, end, 2) as g:
                    quad(g)

            last_of_table = lambda: y_take(T - 1)
            for l in range(L - 1):
                def store_both(t, l=l):
                    for half in range(2):
                        y_store((l + 1) * T + t, t, half, ytab[(l + 1) % 2])

                name_rows(l, 0, last_of_table)
                name_rows(l, 1)
                with act.Fori(2, T) as t:
                    name_rows(l, t)
                    store_both(t - 2)
                store_both(T - 2)
                last_of_table = lambda store=store_both: store(T - 1)

            def last_steps(t):
                def at(lag):
                    return not isinstance(t, int) or 0 <= t - lag < T

                if at(1):
                    rows = LAST if isinstance(t, int) and t - 1 == T - 1 else P
                    if not isinstance(t, int) or t >= 2:
                        act.wait_ge(stats_done, t - 1)
                    act.dma_start(xin[0:rows, 0, :], x[ds((t - 1) * P, rows), :]).then_inc(res_in, 16)
                    act.wait_ge(sum_done, t)
                    nc.scalar.activation(hroot[:, ds(t - 1, 1), :], hroot[:, ds(t - 1, 1), :],
                                         ACT.Sigmoid).then_inc(sig_done, 1)
                if at(2):
                    act.wait_ge(stats_done, t - 1)
                    nc.scalar.activation(std[:, :], mv[:, 1:2], ACT.Sqrt, bias=eps[:, 0:1]).then_inc(std_done, 1)
                if at(3):
                    rows = LAST if isinstance(t, int) and t - 3 == T - 1 else P
                    act.wait_ge(o_ready, t - 2)
                    act.dma_start(out[ds((t - 3) * P, rows), :], o_sb[0:rows, :]).then_inc(o_stored, 16)

            name_rows(L - 1, 0, last_of_table)
            for t in range(1, 4):
                name_rows(L - 1, t)
                last_steps(t)
            with act.Fori(4, T) as t:
                name_rows(L - 1, t)
                last_steps(t)
            for t in range(T, T + 3):
                last_steps(t)
            act.wait_ge(o_stored, 16 * T)

        @block.vector
        def _(dve):
            chain = [0]

            def link(made):
                chain[0] += 1
                made.then_inc(dve_step, 1)
                dve.wait_ge(dve_step, chain[0])

            V = nc.vector
            V.memset(src_r[:, FB * P:CP], 0)
            V.memset(typ_r[:, FB * P:CP], 0)
            V.memset(rowslot[:, :], 0)
            V.memset(ones[:, :], 1.0)
            V.memset(nought[:, :], 0.0)
            V.memset(plan_c[:, :], 0)
            V.memset(eps[:, :], EPS)
            link(V.memset(dst_r[:, FB * P:CP], int(NO_NODE)))
            dve.sem_inc(pads, 1)
            dve.wait_ge(consts_pool, 2)
            V.tensor_scalar(ident[:, :], node_no[:, 0:P], part_no[:, 0:1], None,
                            ALU.is_equal).then_inc(ident_ready, 1)
            V.tensor_scalar(tri[:, :], node_no[:, 0:P], part_no[:, 0:1], None, ALU.is_ge)
            V.tensor_scalar(lo[:, :], part_no[:, :], float(P), None, ALU.mult)
            V.tensor_scalar(hi[:, :], part_no[:, :], float(P), float(P), ALU.mult, ALU.add)
            V.tensor_scalar(v["is_window"][:, :], part_no[:, :], float(T), None, ALU.is_lt)
            V.tensor_scalar(v["is_last"][:, :], part_no[:, :], float(T - 1), None, ALU.is_ge)
            link(V.tensor_scalar(part_1[:, :], part_no[:, :], 1.0, None, ALU.add))
            V.tensor_scalar(shift[:, :], node_no[:, 0:P], part_1[:, 0:1], None, ALU.is_equal)
            dve.wait_ge(consts_pool, 4)
            dve.wait_ge(edges_in, 9 * 16)
            V.scalar_tensor_tensor(rows_f, src_r[:, :], float(R), typ_r[:, :], ALU.mult, ALU.add)
            link(V.tensor_copy(dst_f, dst_r[:, :]))
            dve.sem_inc(edge_rows, 1)
            link(V.scalar_tensor_tensor(dst_v, dst_f, NO_NODE / 2, dst_f, ALU.is_lt, ALU.mult))
            by_chunk = "p (b e) -> p b e"
            V.tensor_reduce(dlow[:, :], dst_f.rearrange(by_chunk, e=P), AXX, ALU.min)
            link(V.tensor_reduce(dhigh[:, :], dst_v.rearrange(by_chunk, e=P), AXX, ALU.max))
            for end, made in ((dlow, spread), (dhigh, spread_hi)):
                V.tensor_tensor(made.rearrange(by_chunk, e=P), ident[:, :].unsqueeze(1).broadcast_to([P, CB, P]),
                                end[:, :].unsqueeze(2).broadcast_to([P, CB, P]), ALU.mult).then_inc(spread_ready, 1)
            for i, to in enumerate((rows_t, dst_t)):
                for b in range(4):
                    dve.wait_ge(tr_ready, 4 * i + b + 1)
                    w = min(COLS, CP - b * COLS)
                    V.tensor_copy(to[:, b * COLS:b * COLS + w], bank[4 * i + b][:, 0:w]).then_inc(tr_taken, 1)
            for b in range(4):
                dve.wait_ge(span_ready, b + 1)
                w = min(COLS, CP - b * COLS)
                V.tensor_scalar(reach_lo[:, b * COLS:b * COLS + w], bank[b][:, 0:w], hi[:, 0:1], None,
                                ALU.is_lt).then_inc(span_taken, 1)
            dve.wait_ge(span_taken, 4)
            for b in range(4):
                dve.wait_ge(span_ready, b + 5)
                w = min(COLS, CP - b * COLS)
                V.scalar_tensor_tensor(reach[:, b * COLS:b * COLS + w], bank[4 + b][:, 0:w], lo[:, 0:1],
                                       reach_lo[:, b * COLS:b * COLS + w], ALU.is_ge, ALU.mult).then_inc(span_taken, 1)
            dve.wait_ge(span_taken, 8)
            link(V.tensor_tensor(reach_lo, reach, chunk_no, ALU.mult))
            link(V.tensor_reduce(v["last_1"][:, :], reach_lo, AXX, ALU.max))
            link(V.tensor_scalar(spread, chunk_no, -1.0, FAR + 1, ALU.mult, ALU.add))
            link(V.tensor_tensor(reach_lo, reach, spread, ALU.mult))
            link(V.tensor_reduce(v["from_end"][:, :], reach_lo, AXX, ALU.max))
            link(V.tensor_scalar(v["first_far"][:, :], v["from_end"][:, :], -1.0, FAR, ALU.mult, ALU.add))
            link(V.tensor_scalar(v["first"][:, :], v["first_far"][:, :], float(C - 1), None, ALU.min))
            link(V.scalar_tensor_tensor(v["last"][:, :], v["last_1"][:, :], -1.0, v["first"][:, :], ALU.add, ALU.max))
            V.tensor_copy(vi["i0"][:, :], v["first"][:, :])
            link(V.tensor_copy(vi["i1"][:, :], v["last"][:, :]))
            V.tensor_scalar(vi["i2"][:, :], vi["i0"][:, :], 2, None, ALU.arith_shift_right)
            link(V.tensor_scalar(vi["i3"][:, :], vi["i1"][:, :], 2, None, ALU.arith_shift_right))
            V.tensor_copy(v["end"][:, :], vi["i3"][:, :])
            link(V.tensor_copy(v["first_quad"][:, :], vi["i2"][:, :]))
            link(V.scalar_tensor_tensor(v["last_quad"][:, :], v["first_quad"][:, :], 1.0, v["end"][:, :], ALU.add, ALU.max))
            link(V.tensor_scalar(next_quad[:, :], v["last_quad"][:, :], 1.0, None, ALU.add))
            dve.sem_inc(steps_ready, 1)
            link(V.tensor_tensor(v["many"][:, :], next_quad[:, :], v["first_quad"][:, :], ALU.subtract))
            link(V.tensor_tensor(v["quads"][:, :], v["many"][:, :], v["is_window"][:, :], ALU.mult))
            dve.wait_ge(sum_ready, 1)
            link(V.scalar_tensor_tensor(v["same"][:, :], v["first_quad"][:, :], 1.0, acc[:, 0:1], ALU.add, ALU.is_equal))
            link(V.scalar_tensor_tensor(counts[:, 1:2], v["quads"][:, :], 2.0, v["same"][:, :], ALU.is_ge, ALU.mult))
            link(V.tensor_tensor(counts[:, 0:1], v["quads"][:, :], counts[:, 1:2], ALU.subtract))
            dve.sem_inc(steps_ready, 1)
            dve.wait_ge(sum_ready, 2)
            V.tensor_scalar(v["end"][:, :], acc[:, 2:3], 2.0, None, ALU.mult)
            V.tensor_scalar(plan_c[:, 3:4], acc[:, 3:4], 2.0, None, ALU.mult)
            V.tensor_scalar(v["twice"][:, :], counts[:, 0:1], 2.0, None, ALU.mult)
            link(V.tensor_scalar(v["share"][:, :], counts[:, 1:2], 2.0, None, ALU.mult))
            link(V.tensor_tensor(v["start"][:, :], v["end"][:, :], v["twice"][:, :], ALU.subtract))
            V.tensor_copy(plan_c[:, 4:5], v["start"][:, :])
            V.tensor_tensor(plan_c[:, 0:1], v["start"][:, :], v["share"][:, :], ALU.subtract)
            V.tensor_scalar(plan_c[:, 2:3], v["first_quad"][:, :], 2.0, None, ALU.mult)
            link(V.tensor_scalar(vi["i4"][:, :], v["end"][:, :], float(PAIRS - 1), None, ALU.add))
            link(V.tensor_scalar(vi["i5"][:, :], vi["i4"][:, :], LOG_PAIRS, LOG_PAIRS, ALU.arith_shift_right, ALU.arith_shift_left))
            link(V.tensor_tensor(v["end_up"][:, :], vi["i5"][:, :], v["end"][:, :], ALU.subtract))
            link(V.tensor_tensor(v["many"][:, :], v["end_up"][:, :], v["is_last"][:, :], ALU.mult))
            link(V.tensor_tensor(plan_c[:, 1:2], v["many"][:, :], v["end"][:, :], ALU.add))
            dve.sem_inc(plan_ready, 1)

            dve.wait_ge(plan_in, 16)
            _, steps = totals(dve)

            def one_hots(l, t, between=None, halfway=None):
                first, end, chunk, twice = window(dve, t)
                used = dve.snap(steps * l + twice + (PAIRS - 1))
                nodes = dve.snap(t * P)
                second = dve.snap(first + 2)
                if halfway:
                    middle = dve.snap((end >> 2) << 1)

                def quad(g):
                    c = dve.snap((chunk + (g - first)) * 2)
                    wanted = [dve.snap(g + used + j) for j in range(2)]
                    of = [c, dve.snap(c + 2)]
                    for j in range(2):
                        dve.wait_ge(slots_free, wanted[j])
                        V.tensor_tensor(hot[:, 2 * j:2 * j + 2, :],
                                        node_no[:, ds(nodes, P)].unsqueeze(1).broadcast_to([P, 2, P]),
                                        dst_t[:, column(of[j], 2)].unsqueeze(2).broadcast_to([P, 2, P]),
                                        ALU.is_equal).then_inc(hot_ready, 1)

                if between:
                    between[0]()
                quad(first)
                if between:
                    between[1]()
                if halfway:
                    with dve.Fori(second, middle, 2) as g:
                        quad(g)
                    halfway()
                    second = middle
                with dve.Fori(second, end, 2) as g:
                    quad(g)

            def flat(ap):
                return ap.rearrange("p a d -> p (a d)")

            def layer_sum(l, t, to):
                dve.wait_ge(acc_ready, l * T + t + 1)
                V.tensor_tensor(s_sb[:, :], acc[:, 0:D], flat(hroot[:, ds(t, 1), :]), ALU.add).then_inc(acc_taken, 1)
                dve.wait_ge(acc_taken, l * T + t + 1)
                return V.tensor_tensor(to, s_sb[:, :], bias_all[:, l, :], ALU.add)

            def next_h(l, t):
                layer_sum(l, t, z_sb[:, :]).then_inc(z_ready, 1)
                dve.wait_ge(z_ready, l * T + t + 1)
                V.tensor_scalar(h_sb[:, :], z_sb[:, :], 0.0, None, ALU.max).then_inc(h_ready, 1)

            def empty_products(n):
                for half in range(2):
                    dve.wait_ge(y_stored[half], n * 16)
                    for k in range(half * HG, (half + 1) * HG):
                        dve.wait_ge(y_ready, n * YG + (k + 1))
                        V.tensor_copy(ystage[:, k * COLS:(k + 1) * COLS], ps_y[k][:, :]).then_inc(y_taken, 1)

            def h_t_copy(n, t):
                dve.wait_ge(xt_done, n + 1)
                V.tensor_copy(h_t[:, 0, :, :].rearrange("p k m -> p (k m)"), ps_t[0][:, 0:D]).then_inc(ht_copied, 1)
                V.tensor_copy(flat(hroot[:, ds(t, 1), :]), ps_t[0][:, 0:D]).then_inc(xt_saved, 1)

            dve.wait_ge(bias_ready, 1)
            V.tensor_copy(bias_all[:, 0, :], bank[0][:, 0:D])
            V.tensor_copy(bias_all[:, 1, :], bank[0][:, D:2 * D])
            V.tensor_copy(bias_all[:, 2, :], ps_t[1][:, 0:D]).then_inc(bias_taken, 1)
            def root_tiles(l, begin, stop):
                def back(n, i):
                    V.tensor_copy(h_t[:, i, :, :].rearrange("p k m -> p (k m)"),
                                  flat(hroot[:, ds(n, 1), :])).then_inc(root_in, 1)

                def take(n, i):
                    dve.wait_ge(r_ready, l * T + n + 1)
                    V.tensor_copy(flat(hroot[:, ds(n, 1), :]), ps_root[i][:, 0:D]).then_inc(r_taken, 1)

                if begin == 0:
                    dve.wait_ge(xt_saved, (l + 1) * T)
                    dve.wait_ge(y_ready, (l + 1) * T * YG)
                even = begin + (stop - begin) // 2 * 2
                back(begin, 0)
                back(begin + 1, 1)
                with dve.Fori(begin, even - 2, 2) as n:
                    for i in range(2):
                        take(n + i, i)
                        back(n + i + 2, i)
                take(even - 2, 0)
                if even < stop:
                    back(even, 0)
                take(even - 1, 1)
                if even < stop:
                    take(even, 0)

            def first_window(l):
                root_tiles(l, ROOTS[0], ROOTS[1])
                one_hots(l, 0, halfway=lambda: root_tiles(l, ROOTS[1], ROOTS[2]))
                root_tiles(l, ROOTS[2], ROOTS[3])

            for l in range(L - 1):
                def n(t):
                    return (l + 1) * T + t

                def after_products(t, lag):
                    if lag:
                        empty_products(n(t) - 1)
                    h_t_copy(n(t), t)

                first_window(l)
                one_hots(l, 1, (lambda: next_h(l, 0), lambda: after_products(0, False)))
                with dve.Fori(2, T) as t:
                    one_hots(l, t, (lambda: next_h(l, t - 1), lambda: after_products(t - 1, True)))
                next_h(l, T - 1)
                after_products(T - 1, True)
                empty_products(n(T - 1))

            def last_steps(t):
                def at(lag):
                    return not isinstance(t, int) or 0 <= t - lag < T

                if at(3):
                    dve.wait_ge(std_done, t - 2)
                    if not isinstance(t, int) or t >= 4:
                        dve.wait_ge(o_stored, 16 * (t - 3))
                    V.reciprocal(rstd[:, :], std[:, :]).then_inc(norm_step, 1)
                    dve.wait_ge(norm_step, t - 2)
                    V.tensor_scalar(o_sb[:, :], z_sb[:, :], mv[:, 0:1],
                                    rstd[:, 0:1], ALU.subtract, ALU.mult).then_inc(o_ready, 1)
                if at(2):
                    dve.wait_ge(sig_done, t - 1)
                    dve.wait_ge(res_in, 16 * (t - 1))
                    if not isinstance(t, int) or t >= 3:
                        dve.wait_ge(o_ready, t - 2)
                    V.tensor_tensor(z_sb[:, :], flat(hroot[:, ds(t - 2, 1), :]), xin[:, 0, :],
                                    ALU.add).then_inc(res_done, 1)
                    dve.wait_ge(res_done, t - 1)
                    V.bn_stats(stats[:, :], z_sb[:, :]).then_inc(bn_done, 1)
                    dve.wait_ge(bn_done, t - 1)
                    dve.nop(nofuse=True)
                    V.bn_aggr(mv[:, :], stats[:, :]).then_inc(stats_done, 1)

            def last_sum(t):
                layer_sum(L - 1, t, flat(hroot[:, ds(t, 1), :])).then_inc(sum_done, 1)

            first_window(L - 1)
            for t in range(1, 4):
                one_hots(L - 1, t, (lambda: last_sum(t - 1), lambda: last_steps(t)))
            with dve.Fori(4, T) as t:
                one_hots(L - 1, t, (lambda: last_sum(t - 1), lambda: last_steps(t)))
            last_sum(T - 1)
            for t in range(T, T + 3):
                last_steps(t)

        @block.tensor
        def _(pe):
            mm = nc.tensor.matmul
            pe.sem_inc(slots_free, PAIRS)
            def transposed(given, i):
                for k in range(KD):
                    made = nc.tensor.transpose(ps_t[i][:, k * P:(k + 1) * P], given[:, k * P:(k + 1) * P], ident[:, :])
                made.then_inc(xt_done, 1)

            def x_tile(n, i, again=True):
                pe.wait_ge(x_in[i], 8 * (n - i) + 16)
                if again:
                    pe.wait_ge(xt_saved, n - 1)
                transposed(xin[:, i, :], i)

            def products(n, i, l, again=True):
                pe.wait_ge(ht_copied, n + 1)
                for g in range(YG):
                    if again:
                        pe.wait_ge(y_taken, n * YG + (g + 1 - YG))
                    for k in range(KD):
                        made = mm(ps_y[g][:, :], lhsT=h_t[:, i, k, :], rhs=w_sb[:, l, k, g * COLS:(g + 1) * COLS],
                                  start=(k == 0), stop=(k == KD - 1))
                    made.then_inc(y_ready, 1)

            pe.wait_ge(ident_ready, 1)
            x_tile(0, 0, False)
            pe.wait_ge(w0_in, 16 * (KD + 1))
            products(0, 0, 0, False)
            x_tile(1, 1, False)
            products(1, 1, 0)
            pe.wait_ge(edge_rows, 1)
            pe.wait_ge(y_taken, 2 * YG)
            for i, given in enumerate((rows_f, dst_f)):
                for b in range(CB):
                    made = nc.tensor.transpose(bank[4 * i + b // 4][:, (b % 4) * P:(b % 4 + 1) * P],
                                               given[:, b * P:(b + 1) * P], ident[:, :])
                    if b % 4 == 3 or b == CB - 1:
                        made.then_inc(tr_ready, 1)
            pe.wait_ge(tr_taken, 8)
            for i, given in enumerate((spread, spread_hi)):
                pe.wait_ge(spread_ready, i + 1)
                for b in range(4):
                    w = min(COLS, CP - b * COLS)
                    mm(bank[4 * i + b][:, 0:w], lhsT=ones[:, :], rhs=given[:, b * COLS:b * COLS + w],
                       start=True, stop=True).then_inc(span_ready, 1)
            pe.wait_ge(span_taken, 8)
            x_tile(2, 0)
            x_tile(3, 1)
            products(2, 0, 0)
            x_tile(4, 0)
            products(3, 1, 0)
            pe.wait_ge(steps_ready, 1)
            mm(acc[:, 0:1], lhsT=shift[:, :], rhs=next_quad[:, :], start=True, stop=True).then_inc(sum_ready, 1)
            x_tile(5, 1)
            products(4, 0, 0)
            x_tile(6, 0)
            products(5, 1, 0)
            pe.wait_ge(steps_ready, 2)
            mm(acc[:, 2:4], lhsT=tri[:, :], rhs=counts[:, :], start=True, stop=True).then_inc(sum_ready, 1)
            with pe.Fori(6, T - 3, 2) as t:
                x_tile(t + 1, 1)
                products(t, 0, 0)
                x_tile(t + 2, 0)
                products(t + 1, 1, 0)
            x_tile(T - 2, 1)
            products(T - 3, 0, 0)
            x_tile(T - 1, 0)
            products(T - 2, 1, 0)
            products(T - 1, 0, 0)

            def root_tiles(l, begin, stop):
                def tile(n, i, again=True):
                    pe.wait_ge(root_in, l * T + n + 1)
                    if again:
                        pe.wait_ge(r_taken, l * T + n - 1)
                    for k in range(KD):
                        made = mm(ps_root[i][:, 0:D], lhsT=h_t[:, i, k, :], rhs=root_sb[:, l, k, :],
                                  start=(k == 0), stop=(k == KD - 1))
                    made.then_inc(r_ready, 1)

                even = begin + (stop - begin) // 2 * 2
                loop = begin
                if begin == 0:
                    pe.wait_ge(y_taken, (l + 1) * T * YG)
                    tile(0, 0, l > 0)
                    tile(1, 1, l > 0)
                    loop = 2
                with pe.Fori(loop, even, 2) as n:
                    tile(n, 0)
                    tile(n + 1, 1)
                if even < stop:
                    tile(even, 0)

            pe.wait_ge(plan_in, 16)
            pe.wait_ge(bias_in, 16)
            mm(bank[0][:, 0:2 * D], lhsT=ones[0:1, :], rhs=bias_sb[0:1, 0:2 * D], start=True, stop=True)
            mm(ps_t[1][:, 0:D], lhsT=ones[0:1, :], rhs=bias_sb[0:1, 2 * D:3 * D],
               start=True, stop=True).then_inc(bias_ready, 1)
            pe.wait_ge(bias_taken, 1)
            total, steps = totals(pe)

            def add_steps(l, t, meanwhile=None, halfway=None):
                if meanwhile:
                    meanwhile()
                first, end, twice = planned(pe, t, 0), planned(pe, t, 1, 2), planned(pe, t, 3)
                step = pe.snap(steps * l + twice)
                before = pe.snap(total * l + 2)
                mm(acc[:, 0:D], lhsT=nought[0:1, 0:P], rhs=nought[0:1, :], start=True, stop=False)
                def quad(g):
                    at = pe.snap((g & (PAIRS - 2)) * (2 * D))
                    of = [at] + [pe.snap(at + i * D) for i in range(1, 4)]
                    wanted = [pe.snap(g + step + (j + 1)) for j in range(2)]
                    pe.wait_ge(arrived, g + before)
                    for i in range(4):
                        if i % 2 == 0:
                            pe.wait_ge(hot_ready, wanted[i // 2])
                        made = mm(acc[:, 0:D], lhsT=hot[:, i, :], rhs=gath_flat[:, ds(of[i], D)],
                                  start=False, stop=False)
                        if i % 2:
                            made.then_inc(slots_free, 1)

                if halfway:
                    middle = pe.snap((end >> 2) << 1)
                    with pe.Fori(first, middle, 2) as g:
                        quad(g)
                    halfway()
                    first = middle
                with pe.Fori(first, end, 2) as g:
                    quad(g)
                mm(acc[:, 0:D], lhsT=nought[0:1, 0:P], rhs=nought[0:1, :], start=False, stop=True).then_inc(acc_ready, 1)

            def first_window(l):
                root_tiles(l, ROOTS[0], ROOTS[1])
                add_steps(l, 0, halfway=lambda: root_tiles(l, ROOTS[1], ROOTS[2]))
                root_tiles(l, ROOTS[2], ROOTS[3])

            def transpose_h(l, t):
                pe.wait_ge(h_ready, l * T + t + 1)
                pe.wait_ge(xt_saved, (l + 1) * T + t)
                transposed(h_sb, 0)

            for l in range(L - 1):
                def n(t):
                    return (l + 1) * T + t

                def between(t):
                    products(n(t) - 1, 0, l + 1)
                    transpose_h(l, t)

                first_window(l)
                if l == 0:
                    pe.wait_ge(late_in, 16 * (L - 1) * (KD * R + 1))
                add_steps(l, 1, lambda: transpose_h(l, 0))
                with pe.Fori(2, T) as t:
                    add_steps(l, t, lambda: between(t - 1))
                between(T - 1)
                products(n(T - 1), 0, l + 1)
            first_window(L - 1)
            with pe.Fori(1, T) as t:
                pe.wait_ge(acc_taken, (L - 1) * T + t)
                add_steps(L - 1, t)


_INS = ['x', 'src', 'dst', 'edge_type_8', 'L0_gnn_weights', 'L0_gnn_roots', 'L0_gnn_biases']


def kernel(**inputs):
    import numpy as _np
    import concourse.bacc as _bacc
    from concourse import mybir as _mybir
    from concourse.bass_utils import run_bass_kernel_spmd as _run

    nc = _bacc.Bacc("TRN2", target_bir_lowering=False, num_devices=1)
    arrays, args = {}, []
    for name in _INS:
        a = _np.ascontiguousarray(inputs[name])
        arrays[f"in_{name}"] = a
        args.append(nc.dram_tensor(f"in_{name}", a.shape, _mybir.dt.from_np(a.dtype), kind="ExternalInput").ap())
    out = nc.dram_tensor("out_0", inputs['x'].shape, _mybir.dt.float32, kind="ExternalOutput").ap()
    relational_graph_layers(nc, *args, out)
    r = _run(nc, [arrays], core_ids=[0])
    return r.results[0]["out_0"]
```
